# Optimizing a Trainium2 kernel written in Bass

```python
import numpy as np
import jax
import jax.numpy as jnp

def _softmax(x, axis=-1):
    return jax.nn.softmax(x, axis=axis)

def _gelu(x):
    return jax.nn.gelu(x, approximate=True)

def _silu(x):
    return jax.nn.silu(x)

def _sigmoid(x):
    return jax.nn.sigmoid(x)

def _layernorm(x, axis=-1, eps=1e-05):
    m = jnp.mean(x, axis=axis, keepdims=True)
    v = jnp.var(x, axis=axis, keepdims=True)
    return (x - m) / jnp.sqrt(v + eps)

def _scatter_add(tgt, idx, src, axis=0):
    return tgt.at[idx].add(src)

def _segment_sum(src, seg, n):
    return jax.ops.segment_sum(src, seg, n)
kernel_name = 'mk_gnn_resnorm_d2_gnn_r32_5ad5a2'

def setup_inputs(seed: int=0):
    np.random.seed(seed)
    _w = jnp.asarray

    def _rec_inputs():
        import jax
        import jax.numpy as jnp
        _gk = jax.random.key(seed)
        x = -0.0008691 + 1 * jax.random.normal(jax.random.fold_in(_gk, 1), (50000, 128), jnp.float32)
        src = jax.random.randint(jax.random.fold_in(_gk, 2), (50000,), 0, 50000, jnp.int32)
        dst = jnp.minimum((50000 * jax.random.uniform(jax.random.fold_in(_gk, 3), (50000,)) ** 2.0).astype(jnp.int32), 49999)
        _o = jnp.argsort(dst, stable=True)
        src = src[_o]
        dst = dst[_o]
        edge_attr_128 = 0.000167468 + 1.0002 * jax.random.normal(jax.random.fold_in(_gk, 11), (50000, 128), jnp.float32)
        return (x, src, dst, edge_attr_128)
    x, src, dst, edge_attr_128 = _rec_inputs()

    def _L0_gnn_setup():
        import jax, jax.numpy as jnp
        import numpy as np
        N_NODES = 10000
        N_EDGES = 20000
        IN_DIM = 128
        OUT_DIM = 128
        key = jax.random.key(seed)
        k1, k2, k3 = jax.random.split(key, 3)
        x = jax.random.normal(k1, (N_NODES, IN_DIM), dtype=jnp.float32)
        edge_index = jax.random.randint(k2, (2, N_EDGES), 0, N_NODES, dtype=jnp.int64)
        W = jax.random.normal(k3, (IN_DIM, OUT_DIM), dtype=jnp.float32) * (1.0 / np.sqrt(IN_DIM))
        b = jnp.zeros((OUT_DIM,), dtype=jnp.float32)
        return {'x': x, 'edge_index': edge_index, 'W': W, 'b': b}
    _L0_gnn_all = _L0_gnn_setup()
    _L0_gnn_in = {k: v for k, v in _L0_gnn_all.items() if k in ('W', 'b')}
    del _L0_gnn_all

    def _L1_gnn_setup():
        import jax, jax.numpy as jnp
        import numpy as np
        N_NODES = 625
        N_EDGES = 10000
        D = 128
        LN_EPS = 1e-05
        key = jax.random.key(seed)
        k1, k2, k3, k4 = jax.random.split(key, 4)
        x = jax.random.normal(k1, (N_NODES, D), dtype=jnp.float32)
        edge_index = jax.random.randint(k2, (2, N_EDGES), 0, N_NODES, dtype=jnp.int64)
        edge_attr = jax.random.normal(k3, (N_EDGES, D), dtype=jnp.float32)
        W = jax.random.normal(k4, (3 * D, D), dtype=jnp.float32) / np.sqrt(3 * D)
        b = jnp.zeros((D,), dtype=jnp.float32)
        gamma = jnp.ones((D,), dtype=jnp.float32)
        beta = jnp.zeros((D,), dtype=jnp.float32)
        return {'x': x, 'edge_index': edge_index, 'edge_attr': edge_attr, 'W': W, 'b': b, 'gamma': gamma, 'beta': beta}
    _L1_gnn_all = _L1_gnn_setup()
    _L1_gnn_in = {k: v for k, v in _L1_gnn_all.items() if k in ('W', 'b', 'gamma', 'beta')}
    del _L1_gnn_all
    return {'x': x, 'src': src, 'dst': dst, 'edge_attr_128': edge_attr_128, 'L0_gnn_W': _L0_gnn_in['W'], 'L0_gnn_b': _L0_gnn_in['b'], 'L1_gnn_W': _L1_gnn_in['W'], 'L1_gnn_b': _L1_gnn_in['b'], 'L1_gnn_gamma': _L1_gnn_in['gamma'], 'L1_gnn_beta': _L1_gnn_in['beta']}

def reference(x, src, dst, edge_attr_128, L0_gnn_W, L0_gnn_b, L1_gnn_W, L1_gnn_b, L1_gnn_gamma, L1_gnn_beta):
    import jax
    import jax.numpy as jnp

    def _L0_gnn_ref(x, edge_index, W, b):
        import jax, jax.numpy as jnp
        import numpy as np
        N_NODES = 10000
        N_EDGES = 20000
        IN_DIM = 128
        OUT_DIM = 128
        n = x.shape[0]
        loop = jnp.arange(n, dtype=edge_index.dtype)
        src = jnp.concatenate([edge_index[0], loop])
        dst = jnp.concatenate([edge_index[1], loop])
        xw = x @ W
        ones = jnp.ones(dst.shape, dtype=x.dtype)
        deg = jax.ops.segment_sum(ones, dst, num_segments=n)
        dinv = jnp.where(deg > 0, jax.lax.rsqrt(deg), 0.0)
        norm = dinv[src] * dinv[dst]
        msg = xw[src] * norm[:, None]
        out = jax.ops.segment_sum(msg, dst, num_segments=n) + b
        return jax.nn.relu(out)

    def _L1_gnn_ref(x, edge_index, edge_attr, W, b, gamma, beta):
        import jax, jax.numpy as jnp
        import numpy as np
        N_NODES = 625
        N_EDGES = 10000
        D = 128
        LN_EPS = 1e-05
        row, col = (edge_index[0], edge_index[1])
        msg_in = jnp.concatenate([x[row], x[col], edge_attr], axis=-1)
        h = msg_in @ W + b
        mu = jnp.mean(h, axis=-1, keepdims=True)
        var = jnp.mean(jnp.square(h - mu), axis=-1, keepdims=True)
        h = (h - mu) * jax.lax.rsqrt(var + LN_EPS) * gamma + beta
        msg = jax.nn.relu(h)
        out = jax.ops.segment_sum(msg, row, num_segments=x.shape[0])
        return out
    edge_index = jnp.stack([src, dst])
    x = _layernorm(x + _L0_gnn_ref(x, edge_index, L0_gnn_W, L0_gnn_b), axis=-1)
    x = _layernorm(x + _L1_gnn_ref(x, edge_index, edge_attr_128, L1_gnn_W, L1_gnn_b, L1_gnn_gamma, L1_gnn_beta), axis=-1)
    return x

_drawn_inputs = setup_inputs


def setup_inputs(seed=0):
    import zlib

    import numpy as np

    out = dict(_drawn_inputs(seed))
    spreads = {'L0_gnn_b': (0.0, 0.1),
     'L1_gnn_b': (0.0, 0.1),
     'L1_gnn_gamma': (1.0, 0.2),
     'L1_gnn_beta': (0.0, 0.1)}
    factors = {}
    for name, (base, spread) in spreads.items():
        noise = np.random.default_rng([zlib.crc32(name.encode()), seed]).standard_normal(out[name].shape)
        drawn = base * np.exp(spread * noise) if base else spread * noise
        out[name] = jnp.asarray(drawn.astype(out[name].dtype))
    for name, factor in factors.items():
        out[name] = (out[name] * factor).astype(out[name].dtype)
    return out
```

```python
from contextlib import ExitStack

import concourse.bass as bass
from concourse import mybir

F32 = mybir.dt.float32
F16 = mybir.dt.float16
I32 = mybir.dt.int32
ALU = mybir.AluOpType
ACT = mybir.ActivationFunctionType

P = 128
EPS = 1e-5
ROWS = 8
HALF = 4
LOG_ROWS = 3
LOG_CHUNK = 10


def program(nc, x, src, dst, edge_attr, w0, b0, w1, b1, gamma, beta, out):
    n_nodes, D = x.shape
    n_edges = src.shape[0]
    chunk = P * ROWS
    chunks = -(-n_nodes // chunk)
    cols = chunks * ROWS
    tail_rows = n_nodes - (chunks - 1) * chunk
    tail_p = tail_rows // ROWS
    assert tail_p * ROWS == tail_rows and chunks % 2 == 1
    spare = -(-n_nodes // P) * P
    table_rows = spare + P
    tiles = -(-n_edges // (2 * HALF * P)) * 2 * HALF
    rounds = tiles // (2 * HALF)
    full_tiles, tail_edges = divmod(n_edges, P)
    assert D == P and cols * P == table_rows and cols <= 512

    def dram(name, rows=table_rows):
        return nc.dram_tensor(name, (rows, D), F32, kind="Internal").ap()

    g_dram, p_dram, q_dram, x1_dram = (dram(n, n_nodes) for n in ("g_dram", "p_dram", "q_dram", "x1_dram"))
    agg = [dram("agg_even"), dram("agg_odd")]
    osum = [dram("osum_even"), dram("osum_odd")]

    with ExitStack() as ctx:
        def sb(name, shape, dt=F32):
            return ctx.enter_context(nc.sbuf_tensor(name, shape, dt))

        def psum(name, shape=(P, HALF, P)):
            return ctx.enter_context(nc.psum_tensor(name, list(shape), F32))

        def sem(name):
            return ctx.enter_context(nc.semaphore(name))

        def sems(name, n):
            return [sem(f"{name}{k}") for k in range(n)]

        ident = sb("ident", [P, P])
        earlier = sb("earlier", [P, P])
        zeros = sb("zeros", [P, ROWS * D])
        iota_i = sb("iota_i", [P, cols], I32)
        iota_h = sb("iota_h", [P, cols], F16)
        spare_i = sb("spare_i", [P, 1], I32)
        spare_f = sb("spare_f", [P, HALF])
        w0_sb = sb("w0_sb", [P, D])
        wab_sb = sb("wab_sb", [P, 2, D])
        wc_sb = sb("wc_sb", [P, D])
        b0_sb = sb("b0_sb", [P, D])
        b1_sb = sb("b1_sb", [P, D])
        gamma_sb = sb("gamma_sb", [P, D])
        beta_sb = sb("beta_sb", [P, D])
        eps_sb = sb("eps_sb", [P, 1])
        row_i = [sb("src_row_i", [P, HALF, P], I32), sb("dst_row_i", [P, HALF, P], I32)]
        row_f = [sb("src_row_f", [P, HALF, P]), sb("dst_row_f", [P, HALF, P])]
        key = [sb("src_key", [P, HALF * P]), sb("dst_key", [P, HALF * P])]
        safe = [sb("src_safe", [P, tiles], I32), sb("dst_safe", [P, tiles], I32)]
        dst_i = sb("dst_i", [P, tiles], I32)
        place_i = sb("place_i", [P, 3, tiles], I32)
        place = sb("place", [P, 2, tiles])
        dinv = sb("dinv", [P, cols])
        root = sb("root", [P, cols])
        xin = [sb(f"xin{k}", [P, ROWS, D]) for k in range(2)]
        ain = [sb(f"ain{k}", [P, ROWS, D]) for k in range(2)]
        bin_ = [sb(f"bin{k}", [P, ROWS, D]) for k in range(2)]
        dout = [sb(f"dout{k}", [P, ROWS, D]) for k in range(2)]
        pout = [sb(f"pout{k}", [P, ROWS, D]) for k in range(2)]
        qout = [sb(f"qout{k}", [P, ROWS, D]) for k in range(2)]
        turned = [sb(f"turned{k}", [P, HALF, P]) for k in range(2)]
        turned1 = [sb(f"turned1_{k}", [P, HALF, P]) for k in range(2)]
        stats = sb("stats", [P, ROWS, 6])
        mean = sb("mean", [P, ROWS])
        spread = sb("spread", [P, ROWS])
        tmp = sb("tmp", [P, 4, ROWS])
        dev = sb("dev", [P, ROWS])
        rstd = sb("rstd", [P, ROWS])
        hot_p = [sb(f"hot_p{k}", [P, P], F16) for k in range(HALF)]
        hot_c = [sb(f"hot_c{k}", [P, cols], F16) for k in range(HALF)]
        key_s = [sb(f"key_s{g}", [P, HALF]) for g in range(2)]
        take_a = [sb(f"take_a{g}", [P, HALF], I32) for g in range(2)]
        take_b = [sb(f"take_b{g}", [P, HALF], I32) for g in range(2)]
        give = [sb(f"give{g}", [P, HALF], I32) for g in range(2)]
        same = [sb(f"same{g}", [P, HALF, P]) for g in range(2)]
        junk = sb("junk", [P, HALF, P])
        before = sb("before", [P, HALF])
        to_spare = sb("to_spare", [P, HALF])
        got_a = [[sb(f"got_a{g}_{k}", [P, D]) for k in range(HALF)] for g in range(2)]
        got_b = [[sb(f"got_b{g}_{k}", [P, D]) for k in range(HALF)] for g in range(2)]
        ea = [sb(f"ea{g}", [P, HALF, D]) for g in range(2)]
        ea_t = [sb(f"ea_t{g}", [P, HALF, P]) for g in range(2)]
        hid = [sb(f"hid{g}", [P, HALF, D]) for g in range(2)]
        hid2 = [sb(f"hid2{g}", [P, HALF, D]) for g in range(2)]
        msg = [sb(f"msg{g}", [P, HALF, D]) for g in range(2)]
        total = [sb(f"total{g}", [P, HALF, D]) for g in range(2)]
        e_stats = sb("e_stats", [P, HALF, 6])
        e_mean = sb("e_mean", [P, HALF])
        e_spread = sb("e_spread", [P, HALF])
        e_tmp = sb("e_tmp", [P, 4, HALF])
        e_dev = sb("e_dev", [P, HALF])
        e_rstd = sb("e_rstd", [P, HALF])

        bank = [psum(f"bank{k}") for k in range(8)]
        count_ps = bank[0][:, :, :].rearrange("p a b -> p (a b)")[:, 0:cols]

        s_iota, s_const, s_zero = sem("s_iota"), sem("s_const"), sem("s_zero")
        s_weights = sem("s_weights")
        s_issued = sem("s_issued")
        s_rows = sem("s_rows")
        s_rowf, s_turn_key, s_key, s_place = sem("s_rowf"), sem("s_turn_key"), sem("s_key"), sem("s_place")
        s_dve = sem("s_dve")
        s_hot, s_counted = sem("s_hot"), sem("s_counted")
        s_root, s_dinv = sem("s_root"), sem("s_dinv")
        s_fill = sems("s_fill", 2)
        b_x, b_g, b_st = sems("b_x", 2), sem("b_g"), sems("b_st", 2)
        d_mom, e_mom, f_mom = sem("d_mom"), sem("e_mom"), sem("f_mom")
        c_stage, c_got, c_turn, c_same = sem("c_stage"), sems("c_got", 8), sem("c_turn"), sem("c_same")
        c_cnt, c_idx, c_sum, c_total, c_put = sem("c_cnt"), sem("c_idx"), sem("c_sum"), sem("c_total"), sems("c_put", 8)
        d_in = sems("d_in", 2)
        d_add, d_turn, d_turned, d_z, d_pre, d_step, d_stat, d_dev, d_x1 = (
            sem(n) for n in ("d_add", "d_turn", "d_turned", "d_z", "d_pre", "d_step", "d_stat", "d_dev", "d_x1"))
        d_turn1, d_turned1, d_pq, d_p, d_q, d_st = (
            sem("d_turn1"), sem("d_turned1"), sem("d_pq"), sem("d_p"), sem("d_q"), sems("d_st", 2))
        e_ea = sems("e_ea", 2)
        e_stage, e_got, e_turn, e_same, e_cnt, e_idx = (
            sem("e_stage"), sems("e_got", 8), sem("e_turn"), sem("e_same"), sem("e_cnt"), sem("e_idx"))
        e_eat, e_ready, e_h, e_stat, e_mvs, e_devs, e_rstds = (
            sem(n) for n in ("e_eat", "e_ready", "e_h", "e_stat", "e_mvs", "e_devs", "e_rstds"))
        e_scaled, e_norm, e_msg, e_sum, e_total, e_put = (
            sem("e_scaled"), sem("e_norm"), sem("e_msg"), sem("e_sum"), sem("e_total"), sems("e_put", 8))
        f_in = sems("f_in", 2)
        f_add, f_res, f_stat, f_agg, f_dev, f_rstd, f_out, f_st = (
            sem("f_add"), sem("f_res"), sem("f_stat"), sem("f_agg"), sem("f_dev"), sem("f_rstd"), sem("f_out"),
            sems("f_st", 2))

        def moments(dve, st, mean, spread, tmp, n, done, at):
            m0, v0, m1, v1 = (st[:, 0:n, c] for c in (1, 2, 4, 5))
            nc.vector.tensor_tensor(tmp[:, 0, 0:n], m0, m1, ALU.add)
            nc.vector.tensor_tensor(tmp[:, 1, 0:n], m0, m1, ALU.subtract)
            nc.vector.tensor_tensor(tmp[:, 2, 0:n], v0, v1, ALU.add).then_inc(done, 1)
            dve.wait_ge(done, at + 1)
            nc.vector.tensor_scalar(mean[:, 0:n], tmp[:, 0, 0:n], 0.5, None, ALU.mult)
            nc.vector.tensor_tensor(tmp[:, 3, 0:n], tmp[:, 1, 0:n], tmp[:, 1, 0:n], ALU.mult).then_inc(done, 1)
            dve.wait_ge(done, at + 2)
            return nc.vector.scalar_tensor_tensor(out=spread[:, 0:n], in0=tmp[:, 3, 0:n], scalar=D / 4.0,
                                                  in1=tmp[:, 2, 0:n], op0=ALU.mult, op1=ALU.add)

        def node_rows(table, c, tail=False):
            if tail:
                return table[n_nodes - tail_rows:n_nodes, :].rearrange("(p r) d -> p r d", r=ROWS)
            return table[bass.ds(c * chunk, chunk), :].rearrange("(p r) d -> p r d", r=ROWS)

        def over_chunks(eng, step):
            with eng.Fori(0, chunks // 2) as i:
                step(0, i)
                step(1, i)
            step(0, chunks // 2)

        def over_groups(eng, step, ahead=None):
            ahead = ahead or (lambda g, r: None)
            ahead(0, 0)
            with eng.Fori(0, rounds - 1) as i:
                ahead(1, i)
                step(0, i)
                ahead(0, i + 1)
                step(1, i)
            ahead(1, rounds - 1)
            step(0, rounds - 1)
            step(1, rounds - 1)

        def group_no(g, r):
            return r * 2 + g

        block = ctx.enter_context(nc.Block())

        @block.sync
        def _(sp):
            sp.wait_ge(s_iota, 2)
            n_row = 0
            for side, ids in enumerate((src, dst)):
                for c in range(HALF):
                    t0, t1 = c * P, min((c + 1) * P, full_tiles)
                    sp.dma_start(row_i[side][0:t1 - t0, c, :],
                                 ids[t0 * P:t1 * P].rearrange("(t e) -> t e", e=P)).then_inc(s_rows, 16)
                    n_row += 1
                at = full_tiles % P
                sp.dma_start(row_i[side][at:at + 1, HALF - 1, 0:tail_edges],
                             ids[full_tiles * P:n_edges].rearrange("(t e) -> t e", t=1)).then_inc(s_rows, 16)
            for to, of in ((w0_sb[:, :], w0), (wab_sb[:, 0, :], w1[0:P, :]), (wab_sb[:, 1, :], w1[P:2 * P, :]),
                           (wc_sb[:, :], w1[2 * P:3 * P, :])):
                sp.dma_start(to, of).then_inc(s_weights, 16)
            for to, of in ((b0_sb, b0), (b1_sb, b1), (gamma_sb, gamma), (beta_sb, beta)):
                sp.dma_start(to[:, :], of.rearrange("(a d) -> a d", a=1).to_broadcast([P, D])).then_inc(s_weights, 16)

            sp.wait_ge(s_zero, 1)
            for n, table in enumerate((agg[1], osum[0], osum[1])):
                with sp.Fori(0, chunks) as i:
                    sp.dma_start(table[bass.ds(i * chunk, chunk), :].rearrange("(p r) d -> p r d", r=ROWS),
                                 zeros[:, :].rearrange("p (r d) -> p r d", d=D)).then_inc(s_fill[0], 16)
            sp.dma_start(agg[0][n_nodes:table_rows, :].rearrange("(p r) d -> p (r d)", r=2),
                         zeros[0:(table_rows - n_nodes) // 2, 0:2 * D]).then_inc(s_fill[1], 16)

            for k in range(2):
                sp.dma_start(xin[k][:, :, :], node_rows(x, k)).then_inc(b_x[k], 16)
            with sp.Fori(1, chunks // 2) as i:
                for k in range(2):
                    sp.wait_ge(b_g, i * 2 + k - 1)
                    sp.dma_start(xin[k][:, :, :], node_rows(x, i * 2 + k)).then_inc(b_x[k], 16)
            sp.wait_ge(b_g, chunks - 2)
            sp.dma_start(xin[0][0:tail_p, :, :], node_rows(x, 0, tail=True)).then_inc(b_x[0], 16)

            for s in c_put:
                sp.wait_ge(s, 16 * rounds)

            def load_d(k, n):
                sp.dma_start(ain[k][:, :, :], node_rows(agg[0], n * 2 + k)).then_inc(d_in[k], 16)
                sp.dma_start(bin_[k][:, :, :], node_rows(agg[1], n * 2 + k)).then_inc(d_in[k], 16)
                sp.dma_start(xin[k][:, :, :], node_rows(x, n * 2 + k)).then_inc(d_in[k], 16)

            load_d(0, 0)
            load_d(1, 0)
            with sp.Fori(1, chunks // 2) as i:
                for k in range(2):
                    sp.wait_ge(d_x1, i * 4 + 2 * k - 2)
                    load_d(k, i)
            sp.wait_ge(d_x1, 2 * (chunks - 2))
            for to, of in ((ain, agg[0]), (bin_, agg[1]), (xin, x)):
                sp.dma_start(to[0][0:tail_p, :, :], node_rows(of, 0, tail=True)).then_inc(d_in[0], 16)

            def load_e(g, r):
                sp.dma_start(ea[g][:, :, :],
                             edge_attr[bass.ds((r * 2 + g) * HALF * P, HALF * P), :].rearrange(
                                 "(k p) d -> p k d", p=P)).then_inc(e_ea[g], 16)

            load_e(0, 0)
            load_e(1, 0)
            with sp.Fori(1, rounds - 1) as i:
                for g in range(2):
                    sp.wait_ge(e_eat, i * 2 + g - 1)
                    load_e(g, i)
            e0 = (rounds - 1) * 2 * HALF * P
            for g in range(2):
                sp.wait_ge(e_eat, (rounds - 1) * 2 + g - 1)
                here = min(HALF, full_tiles - (rounds - 1) * 2 * HALF - g * HALF)
                if here > 0:
                    sp.dma_start(ea[g][:, 0:here, :],
                                 edge_attr[e0 + g * HALF * P:e0 + (g * HALF + here) * P, :].rearrange(
                                     "(k p) d -> p k d", p=P)).then_inc(e_ea[g], 16)
                if 0 <= here < HALF and tail_edges:
                    sp.dma_start(ea[g][0:tail_edges, here, :],
                                 edge_attr[full_tiles * P:n_edges, :]).then_inc(e_ea[g], 16)

            for s in e_put:
                sp.wait_ge(s, 16 * rounds)

            def load_f(k, n):
                sp.dma_start(ain[k][:, :, :], node_rows(osum[0], n * 2 + k)).then_inc(f_in[k], 16)
                sp.dma_start(bin_[k][:, :, :], node_rows(osum[1], n * 2 + k)).then_inc(f_in[k], 16)
                sp.dma_start(xin[k][:, :, :], node_rows(x1_dram, n * 2 + k)).then_inc(f_in[k], 16)

            load_f(0, 0)
            load_f(1, 0)
            with sp.Fori(1, chunks // 2) as i:
                for k in range(2):
                    sp.wait_ge(f_out, i * 2 + k - 1)
                    load_f(k, i)
            sp.wait_ge(f_out, chunks - 2)
            for to, of in ((ain, osum[0]), (bin_, osum[1]), (xin, x1_dram)):
                sp.dma_start(to[0][0:tail_p, :, :], node_rows(of, 0, tail=True)).then_inc(f_in[0], 16)

            sp.wait_ge(f_st[0], 16 * (chunks // 2 + 1))
            sp.wait_ge(f_st[1], 16 * (chunks // 2))

        @block.gpsimd
        def _(pool):
            for side in range(2):
                nc.gpsimd.iota(row_i[side][:, HALF - 1, :], pattern=[[1, P]], base=spare,
                               channel_multiplier=0).then_inc(s_iota, 1)
            nc.gpsimd.iota(iota_i[:, :], pattern=[[1, cols]], base=0, channel_multiplier=0).then_inc(s_iota, 1)
            nc.gpsimd.iota(spare_i[:, :], pattern=[[1, 1]], base=spare, channel_multiplier=1).then_inc(s_iota, 1)
            nc.gpsimd.memset(zeros[:, :], 0.0).then_inc(s_zero, 1)
            nc.gpsimd.memset(ident[:, :], 0.0).then_inc(s_const, 1)
            nc.gpsimd.memset(earlier[:, :], 1.0).then_inc(s_const, 1)
            nc.gpsimd.memset(eps_sb[:, :], EPS).then_inc(s_const, 1)
            pool.wait_ge(s_const, 3)
            nc.gpsimd.affine_select(out=ident[:, :], in_=ident[:, :], compare_op=ALU.not_equal, fill=1.0, base=0,
                                    pattern=[[-1, P]], channel_multiplier=1).then_inc(s_const, 1)
            nc.gpsimd.affine_select(out=earlier[:, :], in_=earlier[:, :], compare_op=ALU.is_gt, fill=0.0, base=0,
                                    pattern=[[-1, P]], channel_multiplier=1).then_inc(s_const, 1)

            pool.wait_ge(b_st[0], 32 * (chunks // 2 + 1))
            pool.wait_ge(b_st[1], 32 * (chunks // 2))
            pool.wait_ge(s_fill[0], 16 * 3 * chunks)
            pool.wait_ge(s_fill[1], 16)

            def take_1(g, r, k):
                if k == 0:
                    pool.wait_ge(c_stage, group_no(g, r) + 1)
                    pool.sem_inc(s_issued, 1)
                nc.gpsimd.indirect_dma_start(
                    got_a[g][k][:, :], None, g_dram, bass.IndirectOffsetOnAxis(take_a[g][:, k:k + 1], 0),
                    bounds_check=n_nodes - 1, oob_is_err=True).then_inc(c_got[g * HALF + k], 16)

            def put_1(g, r, k):
                if k == 0:
                    pool.wait_ge(c_idx, group_no(g, r) + 1)
                    pool.wait_ge(c_total, group_no(g, r) + 1)
                g0, k0 = (g, k - 2) if k >= 2 else (1 - g, k + 2)
                pool.wait_ge(c_put[g0 * HALF + k0], (r + (1 if (g or k >= 2) else 0)) * 16)
                pool.sem_inc(s_issued, 1)
                nc.gpsimd.indirect_dma_start(
                    agg[k % 2], bass.IndirectOffsetOnAxis(give[g][:, k:k + 1], 0), total[g][:, k, :], None,
                    bounds_check=table_rows - 1, oob_is_err=True, compute_op=ALU.add).then_inc(
                        c_put[g * HALF + k], 16)

            def alternate(take, put):
                for k in range(HALF):
                    take(0, 0, k)
                with pool.Fori(0, rounds - 1) as i:
                    for k in range(HALF):
                        take(1, i, k)
                        put(0, i, k)
                    for k in range(HALF):
                        take(0, i + 1, k)
                        put(1, i, k)
                for k in range(HALF):
                    take(1, rounds - 1, k)
                    put(0, rounds - 1, k)
                for k in range(HALF):
                    put(1, rounds - 1, k)

            alternate(take_1, put_1)

            pool.wait_ge(d_st[0], 48 * (chunks // 2 + 1))
            pool.wait_ge(d_st[1], 48 * (chunks // 2))

            def take_2(g, r, k):
                if k == 0:
                    pool.wait_ge(e_stage, group_no(g, r) + 1)
                    pool.sem_inc(s_issued, 1)
                nc.gpsimd.indirect_dma_start(
                    got_a[g][k][:, :], None, p_dram, bass.IndirectOffsetOnAxis(take_a[g][:, k:k + 1], 0),
                    bounds_check=n_nodes - 1, oob_is_err=True).then_inc(e_got[g * HALF + k], 16)
                nc.gpsimd.indirect_dma_start(
                    got_b[g][k][:, :], None, q_dram, bass.IndirectOffsetOnAxis(take_b[g][:, k:k + 1], 0),
                    bounds_check=n_nodes - 1, oob_is_err=True).then_inc(e_got[g * HALF + k], 16)

            def put_2(g, r, k):
                if k == 0:
                    pool.wait_ge(e_idx, group_no(g, r) + 1)
                    pool.wait_ge(e_total, group_no(g, r) + 1)
                g0, k0 = (g, k - 2) if k >= 2 else (1 - g, k + 2)
                pool.wait_ge(e_put[g0 * HALF + k0], (r + (1 if (g or k >= 2) else 0)) * 16)
                pool.sem_inc(s_issued, 1)
                nc.gpsimd.indirect_dma_start(
                    osum[k % 2], bass.IndirectOffsetOnAxis(give[g][:, k:k + 1], 0), total[g][:, k, :], None,
                    bounds_check=table_rows - 1, oob_is_err=True, compute_op=ALU.add).then_inc(
                        e_put[g * HALF + k], 16)

            alternate(take_2, put_2)

        @block.tensor
        def _(pe):
            pe.wait_ge(s_const, 5)
            pe.wait_ge(s_rowf, 2)
            for side in range(2):
                for c in range(HALF):
                    n = min(P, tiles - c * P)
                    last = nc.tensor.transpose(bank[1 + side][:, c, 0:n], row_f[side][0:n, c, :], ident[0:n, 0:n])
                last.then_inc(s_turn_key, 1)

            def count(first, last_one, n):
                for k in range(HALF):
                    pe.wait_ge(s_hot, n * HALF + k + 1)
                    nc.tensor.matmul(count_ps, hot_p[k][:, :], hot_c[k][:, :], start=first and k == 0,
                                     stop=last_one and k == HALF - 1).then_inc(s_counted, 1)

            count(True, False, 0)
            with pe.Fori(1, tiles // HALF - 1) as i:
                count(False, False, i)
            count(False, True, tiles // HALF - 1)

            pe.wait_ge(s_dinv, 1)

            def keys_1(g, r):
                n = group_no(g, r)
                pe.wait_ge(c_stage, n + 1)
                for k in range(HALF):
                    last = nc.tensor.transpose(bank[g][:, k, :], key_s[g][:, k:k + 1].to_broadcast([P, P]),
                                               ident[:, :])
                last.then_inc(c_turn, 1)

            def sum_1(g, r):
                n = group_no(g, r)
                pe.wait_ge(c_same, n + 1)
                for k in range(HALF):
                    pe.wait_ge(c_got[g * HALF + k], r * 16 + 16)
                    last = nc.tensor.matmul(bank[2 + g][:, k, :], same[g][:, k, :], got_a[g][k][:, :],
                                            start=True, stop=True)
                last.then_inc(c_sum, 1)

            over_groups(pe, sum_1, keys_1)

            pe.wait_ge(s_weights, 8 * 16)

            def front(k, n, h):
                u = n * 4 + 2 * k + h
                pe.wait_ge(d_add, n * 2 + k + 1)
                for j in range(HALF):
                    last = nc.tensor.transpose(bank[h][:, j, :], ain[k][:, h * HALF + j, :], ident[:, :])
                last.then_inc(d_turn, 1)
                pe.wait_ge(d_turned, u + 1)
                pe.wait_ge(d_pre, u - 1 if h else u)
                for j in range(HALF):
                    last = nc.tensor.matmul(bank[2 + h][:, j, :], turned[h][:, j, :], w0_sb[:, :], start=True,
                                            stop=True)
                last.then_inc(d_z, 1)

            def back(k, n, h):
                u = n * 4 + 2 * k + h
                pe.wait_ge(d_x1, u + 1)
                for j in range(HALF):
                    last = nc.tensor.transpose(bank[4 + h][:, j, :], dout[k][:, h * HALF + j, :], ident[:, :])
                last.then_inc(d_turn1, 1)
                pe.wait_ge(d_turned1, u + 1)
                pe.wait_ge(d_p, u)
                pe.wait_ge(d_q, u)
                for w in range(2):
                    for j in range(HALF):
                        last = nc.tensor.matmul(bank[6 + w][:, j, :], turned1[h][:, j, :], wab_sb[:, w, :],
                                                start=True, stop=True)
                last.then_inc(d_pq, 1)

            front(0, 0, 0)
            with pe.Fori(0, chunks // 2) as i:
                front(0, i, 1)
                back(0, i, 0)
                front(1, i, 0)
                back(0, i, 1)
                front(1, i, 1)
                back(1, i, 0)
                front(0, i + 1, 0)
                back(1, i, 1)
            front(0, chunks // 2, 1)
            back(0, chunks // 2, 0)
            back(0, chunks // 2, 1)

            def front_2(g, r):
                n = group_no(g, r)
                pe.wait_ge(e_stage, n + 1)
                for k in range(HALF):
                    last = nc.tensor.transpose(bank[g][:, k, :], key_s[g][:, k:k + 1].to_broadcast([P, P]),
                                               ident[:, :])
                last.then_inc(e_turn, 1)
                if isinstance(r, int) and r == rounds - 1:
                    here = full_tiles - (rounds - 1) * 2 * HALF - g * HALF
                    loads = (1 if here > 0 else 0) + (1 if 0 <= here < HALF and tail_edges else 0)
                    pe.wait_ge(e_ea[g], (rounds - 1) * 16 + loads * 16)
                else:
                    pe.wait_ge(e_ea[g], r * 16 + 16)
                for k in range(HALF):
                    last = nc.tensor.transpose(bank[2 + g][:, k, :], ea[g][:, k, :], ident[:, :])
                last.then_inc(e_eat, 1)

            def hidden_2(g, r):
                n = group_no(g, r)
                pe.wait_ge(e_ready, n + 1)
                for k in range(HALF):
                    pe.wait_ge(e_got[g * HALF + k], r * 32 + 32)
                    nc.tensor.matmul(bank[4 + g][:, k, :], ea_t[g][:, k, :], wc_sb[:, :], start=True, stop=False)
                    nc.tensor.matmul(bank[4 + g][:, k, :], ident[:, :], got_a[g][k][:, :], start=False, stop=False)
                    last = nc.tensor.matmul(bank[4 + g][:, k, :], ident[:, :], got_b[g][k][:, :], start=False,
                                            stop=True)
                last.then_inc(e_h, 1)

            def sum_2(g, r):
                n = group_no(g, r)
                pe.wait_ge(e_same, n + 1)
                pe.wait_ge(e_msg, n + 1)
                for k in range(HALF):
                    last = nc.tensor.matmul(bank[6 + g][:, k, :], same[g][:, k, :], msg[g][:, k, :], start=True,
                                            stop=True)
                last.then_inc(e_sum, 1)

            def step_2(g, r):
                hidden_2(g, r)
                sum_2(g, r)

            over_groups(pe, step_2, front_2)

        @block.scalar
        def _(act):
            act.wait_ge(s_counted, tiles)
            nc.scalar.activation(root[:, :], count_ps, ACT.Sqrt, bias=1.0).then_inc(s_root, 1)

            def store_g(k, n, rows=None):
                act.wait_ge(b_g, n * 2 + k + 1)
                for table in (g_dram, agg[0]):
                    act.dma_start(node_rows(table, n * 2 + k, tail=rows is not None),
                                  dout[k][0:rows or P, :, :]).then_inc(b_st[k], 16)

            with act.Fori(0, chunks // 2) as i:
                store_g(0, i)
                store_g(1, i)
            store_g(0, chunks // 2, tail_p)

            def totals_1(g, r):
                n = group_no(g, r)
                act.wait_ge(c_sum, n + 1)
                for k in range(HALF):
                    act.wait_ge(c_put[g * HALF + k], r * 16)
                nc.scalar.copy(total[g][:, :, :], bank[2 + g][:, :, :]).then_inc(c_total, 1)

            with act.Fori(0, rounds) as i:
                totals_1(0, i)
                totals_1(1, i)

            def front(k, n, h):
                u = n * 4 + 2 * k + h
                act.wait_ge(d_turn, u + 1)
                act.wait_ge(d_z, u - 1 if h else u)
                nc.scalar.copy(turned[h][:, :, :], bank[h][:, :, :]).then_inc(d_turned, 1)

            def deviation(k, n, h):
                u = n * 4 + 2 * k + h
                act.wait_ge(d_stat, u + 1)
                act.wait_ge(d_x1, u)
                nc.scalar.activation(dev[:, 0:HALF], spread[:, 0:HALF], ACT.Sqrt, bias=eps_sb[:, :],
                                     scale=1.0 / D).then_inc(d_dev, 1)

            def back(k, n, h):
                u = n * 4 + 2 * k + h
                act.wait_ge(d_turn1, u + 1)
                act.wait_ge(d_pq, u - 1 if h else u)
                nc.scalar.copy(turned1[h][:, :, :], bank[4 + h][:, :, :]).then_inc(d_turned1, 1)
                act.wait_ge(d_pq, u + 1)
                act.wait_ge(d_st[k], n * 48)
                nc.scalar.copy(qout[k][:, h * HALF:(h + 1) * HALF, :], bank[7][:, :, :]).then_inc(d_q, 1)

            def store_d(k, n, rows=None):
                for table, of, done in ((x1_dram, dout, d_x1), (p_dram, pout, d_p), (q_dram, qout, d_q)):
                    act.wait_ge(done, n * 4 + 2 * k + 2)
                    act.dma_start(node_rows(table, n * 2 + k, tail=rows is not None),
                                  of[k][0:rows or P, :, :]).then_inc(d_st[k], 16)

            front(0, 0, 0)
            deviation(0, 0, 0)
            with act.Fori(0, chunks // 2) as i:
                front(0, i, 1)
                back(0, i, 0)
                deviation(0, i, 1)
                front(1, i, 0)
                back(0, i, 1)
                deviation(1, i, 0)
                store_d(0, i)
                front(1, i, 1)
                back(1, i, 0)
                deviation(1, i, 1)
                front(0, i + 1, 0)
                back(1, i, 1)
                deviation(0, i + 1, 0)
                store_d(1, i)
            front(0, chunks // 2, 1)
            back(0, chunks // 2, 0)
            deviation(0, chunks // 2, 1)
            back(0, chunks // 2, 1)
            store_d(0, chunks // 2, tail_p)

            def ready_2(g, r):
                n = group_no(g, r)
                act.wait_ge(e_eat, n + 1)
                act.wait_ge(e_h, n - 1 if g else n)
                nc.scalar.copy(ea_t[g][:, :, :], bank[2 + g][:, :, :]).then_inc(e_ready, 1)

            def messages_2(g, r):
                n = group_no(g, r)
                act.wait_ge(e_mvs, n + 1)
                act.wait_ge(e_norm, n)
                nc.scalar.activation(e_dev[:, :], e_spread[:, :], ACT.Sqrt, bias=eps_sb[:, :],
                                     scale=1.0 / D).then_inc(e_devs, 1)
                act.wait_ge(e_norm, n + 1)
                act.wait_ge(e_sum, n - 1 if g else n)
                nc.scalar.activation(msg[g][:, :, :], hid2[g][:, :, :], ACT.Relu).then_inc(e_msg, 1)
                act.wait_ge(e_sum, n + 1)
                for k in range(HALF):
                    act.wait_ge(e_put[g * HALF + k], r * 16)
                nc.scalar.copy(total[g][:, :, :], bank[6 + g][:, :, :]).then_inc(e_total, 1)

            over_groups(act, messages_2, ready_2)

            def dev_2(k, n):
                c = n * 2 + k
                act.wait_ge(f_agg, c + 1)
                act.wait_ge(f_out, c)
                nc.scalar.activation(dev[:, :], spread[:, :], ACT.Sqrt, bias=eps_sb[:, :],
                                     scale=1.0 / D).then_inc(f_dev, 1)

                act.wait_ge(f_out, c + 1)
                if isinstance(n, int):
                    act.dma_start(node_rows(out, 0, tail=True), dout[k][0:tail_p, :, :]).then_inc(f_st[k], 16)
                else:
                    act.dma_start(node_rows(out, c), dout[k][:, :, :]).then_inc(f_st[k], 16)

            over_chunks(act, dev_2)

        @block.vector
        def _(dve):
            made = [0]

            def link(ins):
                made[0] += 1
                ins.then_inc(s_dve, 1)
                dve.wait_ge(s_dve, made[0])

            dve.wait_ge(s_iota, 4)
            nc.vector.tensor_copy(iota_h[:, :], iota_i[:, :])
            link(nc.vector.tensor_copy(spare_f[:, :], spare_i[:, :].to_broadcast([P, HALF])))
            dve.wait_ge(s_rows, 16 * 2 * (HALF + 1))
            for side in range(2):
                nc.vector.tensor_copy(row_f[side][:, 0:HALF - 1, :], row_i[side][:, 0:HALF - 1, :])
                n = tiles - (HALF - 1) * P
                nc.vector.tensor_copy(row_f[side][0:n, HALF - 1, :],
                                      row_i[side][0:n, HALF - 1, :]).then_inc(s_rowf, 1)
            for side in range(2):
                dve.wait_ge(s_turn_key, side + 1)
                link(nc.vector.tensor_copy(key[side][:, 0:tiles],
                                           bank[1 + side][:, :, :].rearrange("p a b -> p (a b)")[:, 0:tiles]))
                link(nc.vector.tensor_scalar(safe[side][:, :], key[side][:, 0:tiles], float(n_nodes - 1), None,
                                             ALU.min))
            link(nc.vector.tensor_copy(dst_i[:, :], key[1][:, 0:tiles]))
            nc.vector.tensor_scalar(place_i[:, 0, :], dst_i[:, :], LOG_ROWS, P - 1, ALU.arith_shift_right,
                                    ALU.bitwise_and)
            nc.vector.tensor_scalar(place_i[:, 1, :], dst_i[:, :], LOG_CHUNK, None, ALU.arith_shift_right)
            link(nc.vector.tensor_scalar(place_i[:, 2, :], dst_i[:, :], ROWS - 1, None, ALU.bitwise_and))
            nc.vector.tensor_copy(place[:, 0, :], place_i[:, 0, :])
            link(nc.vector.scalar_tensor_tensor(out=place[:, 1, :], in0=place_i[:, 1, :], scalar=float(ROWS),
                                                in1=place_i[:, 2, :], op0=ALU.mult, op1=ALU.add))

            def one_hot(n):
                for k in range(HALF):
                    t = n * HALF + k
                    nc.vector.tensor_scalar(hot_p[k][:, :], iota_h[:, 0:P], place[:, 0, bass.ds(t, 1)], None,
                                            ALU.is_equal)
                    nc.vector.tensor_scalar(hot_c[k][:, :], iota_h[:, :], place[:, 1, bass.ds(t, 1)], None,
                                            ALU.is_equal).then_inc(s_hot, 1)

            one_hot(0)
            with dve.Fori(1, tiles // HALF) as i:
                dve.wait_ge(s_counted, i * HALF)
                one_hot(i)

            dve.wait_ge(s_root, 1)
            nc.vector.reciprocal(dinv[:, :], root[:, :]).then_inc(s_dinv, 1)
            dve.wait_ge(s_dinv, 1)

            def scale(k, n):
                c = n * 2 + k
                dve.wait_ge(b_x[k], n * 16 + 16)
                dve.wait_ge(b_st[k], n * 32)
                for j in range(ROWS):
                    last = nc.vector.tensor_scalar(dout[k][:, j, :], xin[k][:, j, :], dinv[:, bass.ds(c * ROWS + j, 1)],
                                                   None, ALU.mult)
                last.then_inc(b_g, 1)

            over_chunks(dve, scale)

            def stage_1(g, r):
                n = group_no(g, r)
                t = n * HALF
                for k in range(HALF):
                    dve.wait_ge(c_got[g * HALF + k], r * 16)
                if not (isinstance(r, int) and n == 0):
                    dve.wait_ge(c_idx, n - 1)
                nc.vector.tensor_copy(take_a[g][:, :], safe[0][:, bass.ds(t, HALF)])
                nc.vector.tensor_copy(key_s[g][:, :], key[1][:, bass.ds(t, HALF)]).then_inc(c_stage, 1)

            def same_index(g, n, r, turn, done, counted, listed, put):
                dve.wait_ge(turn, n + 1)
                for k in range(HALF):
                    nc.vector.tensor_scalar(same[g][:, k, :], bank[g][:, k, :], key_s[g][:, k:k + 1], None,
                                            ALU.is_equal)
                    last = nc.vector.scalar_tensor_tensor(
                        out=junk[:, k, :], in0=bank[g][:, k, :], scalar=key_s[g][:, k:k + 1], in1=earlier[:, :],
                        op0=ALU.is_equal, op1=ALU.mult)
                last.then_inc(done, 1)
                dve.wait_ge(done, n + 1)
                nc.vector.tensor_reduce(before[:, :], junk[:, :, :], mybir.AxisListType.X, ALU.max).then_inc(counted, 1)
                dve.wait_ge(counted, n * 3 + 1)
                nc.vector.tensor_tensor(to_spare[:, :], spare_f[:, :], key_s[g][:, :], ALU.subtract).then_inc(
                    counted, 1)
                dve.wait_ge(counted, n * 3 + 2)
                nc.vector.tensor_tensor(to_spare[:, :], to_spare[:, :], before[:, :], ALU.mult).then_inc(counted, 1)
                dve.wait_ge(counted, n * 3 + 3)
                for k in range(HALF):
                    dve.wait_ge(put[g * HALF + k], r * 16)
                nc.vector.tensor_tensor(give[g][:, :], to_spare[:, :], key_s[g][:, :], ALU.add).then_inc(listed, 1)

            def step_1(g, r):
                n = group_no(g, r)
                dve.wait_ge(c_sum, n - 1 if g else n)
                same_index(g, n, r, c_turn, c_same, c_cnt, c_idx, c_put)

            over_groups(dve, step_1, stage_1)

            def add_sums(k, n):
                dve.wait_ge(d_in[k], n * 48 + 48)
                nc.vector.tensor_tensor(ain[k][:, :, :], ain[k][:, :, :], bin_[k][:, :, :], ALU.add).then_inc(d_add, 1)

            def half(k, n, h):
                u = n * 4 + 2 * k + h
                c = n * 2 + k
                if h == 0:
                    dve.wait_ge(d_st[k], n * 48)
                dve.wait_ge(d_z, u + 1)
                rows = [h * HALF + j for j in range(HALF)]
                for j in rows:
                    last = nc.vector.scalar_tensor_tensor(
                        out=dout[k][:, j, :], in0=bank[2 + h][:, j - h * HALF, :],
                        scalar=dinv[:, bass.ds(c * ROWS + j, 1)], in1=b0_sb[:, :], op0=ALU.mult, op1=ALU.add)
                last.then_inc(d_pre, 1)
                dve.wait_ge(d_pre, u + 1)
                part = slice(h * HALF, (h + 1) * HALF)
                nc.vector.scalar_tensor_tensor(
                    out=xin[k][:, part, :], in0=dout[k][:, part, :], scalar=0.0, in1=xin[k][:, part, :], op0=ALU.max,
                    op1=ALU.add).then_inc(d_step, 1)
                dve.wait_ge(d_step, u * 3 + 1)
                for j in rows:
                    last = nc.vector.bn_stats(stats[:, j - h * HALF, :], xin[k][:, j, :])
                last.then_inc(d_step, 1)
                dve.wait_ge(d_step, u * 3 + 2)
                moments(dve, stats, mean, spread, tmp, HALF, d_mom, u * 2).then_inc(d_stat, 1)
                dve.wait_ge(d_dev, u + 1)
                nc.vector.reciprocal(rstd[:, 0:HALF], dev[:, 0:HALF]).then_inc(d_step, 1)
                dve.wait_ge(d_step, u * 3 + 3)
                for j in range(HALF):
                    last = nc.vector.tensor_scalar(dout[k][:, h * HALF + j, :], xin[k][:, h * HALF + j, :],
                                                   mean[:, j:j + 1], rstd[:, j:j + 1], ALU.subtract, ALU.mult)
                last.then_inc(d_x1, 1)

            def p_out(k, n, h):
                u = n * 4 + 2 * k + h
                dve.wait_ge(d_pq, u + 1)
                for j in range(HALF):
                    last = nc.vector.tensor_tensor(pout[k][:, h * HALF + j, :], bank[6][:, j, :], b1_sb[:, :], ALU.add)
                last.then_inc(d_p, 1)

            add_sums(0, 0)
            half(0, 0, 0)
            with dve.Fori(0, chunks // 2) as i:
                half(0, i, 1)
                p_out(0, i, 0)
                add_sums(1, i)
                half(1, i, 0)
                p_out(0, i, 1)
                half(1, i, 1)
                p_out(1, i, 0)
                add_sums(0, i + 1)
                half(0, i + 1, 0)
                p_out(1, i, 1)
            half(0, chunks // 2, 1)
            p_out(0, chunks // 2, 0)
            p_out(0, chunks // 2, 1)

            dve.wait_ge(c_idx, 2 * rounds)

            def stage_2(g, r):
                n = group_no(g, r)
                t = n * HALF
                for k in range(HALF):
                    dve.wait_ge(e_got[g * HALF + k], r * 32)
                if not (isinstance(r, int) and n == 0):
                    dve.wait_ge(e_idx, n - 1)
                nc.vector.tensor_copy(take_a[g][:, :], safe[0][:, bass.ds(t, HALF)])
                nc.vector.tensor_copy(take_b[g][:, :], safe[1][:, bass.ds(t, HALF)])
                nc.vector.tensor_copy(key_s[g][:, :], key[0][:, bass.ds(t, HALF)]).then_inc(e_stage, 1)

            def step_2(g, r):
                n = group_no(g, r)
                dve.wait_ge(e_sum, n - 1 if g else n)
                same_index(g, n, r, e_turn, e_same, e_cnt, e_idx, e_put)
                dve.wait_ge(e_h, n + 1)
                for k in range(HALF):
                    last = nc.vector.bn_stats(e_stats[:, k, :], bank[4 + g][:, k, :])
                last.then_inc(e_stat, 1)
                dve.wait_ge(e_stat, n + 1)
                moments(dve, e_stats, e_mean, e_spread, e_tmp, HALF, e_mom, n * 2).then_inc(e_mvs, 1)
                dve.wait_ge(e_mvs, n + 1)
                for k in range(HALF):
                    last = nc.vector.scalar_tensor_tensor(
                        out=hid[g][:, k, :], in0=bank[4 + g][:, k, :], scalar=e_mean[:, k:k + 1], in1=gamma_sb[:, :],
                        op0=ALU.subtract, op1=ALU.mult)
                last.then_inc(e_scaled, 1)
                dve.wait_ge(e_devs, n + 1)
                nc.vector.reciprocal(e_rstd[:, :], e_dev[:, :]).then_inc(e_rstds, 1)
                dve.wait_ge(e_rstds, n + 1)
                dve.wait_ge(e_scaled, n + 1)
                dve.wait_ge(e_msg, n - 1 if g else n)
                for k in range(HALF):
                    last = nc.vector.scalar_tensor_tensor(
                        out=hid2[g][:, k, :], in0=hid[g][:, k, :], scalar=e_rstd[:, k:k + 1], in1=beta_sb[:, :],
                        op0=ALU.mult, op1=ALU.add)
                last.then_inc(e_norm, 1)

            over_groups(dve, step_2, stage_2)

            def x2(k, n):
                c = n * 2 + k
                dve.wait_ge(f_in[k], n * 48 + 48)
                nc.vector.tensor_tensor(ain[k][:, :, :], ain[k][:, :, :], bin_[k][:, :, :], ALU.add).then_inc(f_add, 1)
                dve.wait_ge(f_add, c + 1)
                nc.vector.tensor_tensor(ain[k][:, :, :], ain[k][:, :, :], xin[k][:, :, :], ALU.add).then_inc(f_res, 1)
                dve.wait_ge(f_res, c + 1)
                for j in range(ROWS):
                    last = nc.vector.bn_stats(stats[:, j, :], ain[k][:, j, :])
                last.then_inc(f_stat, 1)
                dve.wait_ge(f_stat, c + 1)
                moments(dve, stats, mean, spread, tmp, ROWS, f_mom, c * 2).then_inc(f_agg, 1)
                dve.wait_ge(f_dev, c + 1)
                nc.vector.reciprocal(rstd[:, :], dev[:, :]).then_inc(f_rstd, 1)
                dve.wait_ge(f_rstd, c + 1)
                dve.wait_ge(f_st[k], n * 16)
                for j in range(ROWS):
                    last = nc.vector.tensor_scalar(dout[k][:, j, :], ain[k][:, j, :], mean[:, j:j + 1],
                                                   rstd[:, j:j + 1], ALU.subtract, ALU.mult)
                last.then_inc(f_out, 1)

            over_chunks(dve, x2)


_INS = ["x", "src", "dst", "edge_attr_128", "L0_gnn_W", "L0_gnn_b", "L1_gnn_W", "L1_gnn_b", "L1_gnn_gamma",
        "L1_gnn_beta"]


def kernel(**inputs):
    import numpy as np
    import concourse.bacc as bacc
    from concourse import mybir as _mybir
    from concourse.bass_utils import run_bass_kernel_spmd

    nc = bacc.Bacc("TRN2", target_bir_lowering=False, num_devices=1)
    arrays, args = {}, []
    for name in _INS:
        a = np.ascontiguousarray(inputs[name])
        arrays[f"in_{name}"] = a
        args.append(nc.dram_tensor(f"in_{name}", a.shape, _mybir.dt.from_np(a.dtype), kind="ExternalInput").ap())
    result = nc.dram_tensor("out_x", inputs["x"].shape, _mybir.dt.float32, kind="ExternalOutput").ap()
    program(nc, *args, result)
    r = run_bass_kernel_spmd(nc, [arrays], core_ids=[0])
    return r.results[0]["out_x"]
```

```python
from contextlib import ExitStack

import concourse.bass as bass
from concourse import mybir

F32 = mybir.dt.float32
F16 = mybir.dt.float16
BF16 = mybir.dt.bfloat16
I32 = mybir.dt.int32
ALU = mybir.AluOpType
ACT = mybir.ActivationFunctionType

P = 128
EPS = 1e-5
ROWS = 8
HALF = 4
SLOTS = 6
HOTS = 8
DEEP = 4
BY_ACT = 2
LOG_ROWS = 3
LOG_CHUNK = 10


def program(nc, x, src, dst, edge_attr, w0, b0, w1, b1, gamma, beta, out):
    n_nodes, D = x.shape
    n_edges = src.shape[0]
    chunk = P * ROWS
    chunks = -(-n_nodes // chunk)
    cols = chunks * ROWS
    tail_rows = n_nodes - (chunks - 1) * chunk
    tail_p = tail_rows // ROWS
    assert tail_p * ROWS == tail_rows and chunks % 2 == 1
    spare = -(-n_nodes // P) * P
    table_rows = spare + (1 + HALF) * P
    tiles = -(-n_edges // (2 * HALF * P)) * 2 * HALF
    rounds = tiles // (2 * HALF)
    full_tiles, tail_edges = divmod(n_edges, P)
    assert D == P and cols * P == spare + P and cols <= 512

    def dram(name, rows=table_rows):
        return nc.dram_tensor(name, (rows, D), F32, kind="Internal").ap()

    x1_dram = dram("x1_dram", n_nodes)
    agg, osum = dram("agg"), dram("osum")

    with ExitStack() as ctx:
        def sb(name, shape, dt=F32):
            return ctx.enter_context(nc.sbuf_tensor(name, shape, dt))

        def psum(name, shape=(P, HALF, P)):
            return ctx.enter_context(nc.psum_tensor(name, list(shape), F32))

        def sem(name):
            return ctx.enter_context(nc.semaphore(name))

        def sems(name, n):
            return [sem(f"{name}{k}") for k in range(n)]

        ident = sb("ident", [P, P])
        earlier = sb("earlier", [P, HALF * P])
        zeros = sb("zeros", [P, ROWS * D])
        iota_i = sb("iota_i", [P, cols], I32)
        iota_h = sb("iota_h", [P, cols], F16)
        spare_i = sb("spare_i", [P, HALF], I32)
        spare_f = sb("spare_f", [P, HALF])
        own_i = sb("own_i", [P, 1], I32)
        own_f = sb("own_f", [P, 1])
        w0_sb = sb("w0_sb", [P, D])
        w1_sb = sb("w1_sb", [P, 3, D])
        bias_hi = sb("bias_hi", [3, HALF, D], BF16)
        bias_row = [sb(f"bias_row{n}", [3, HALF, D], BF16) for n in range(2)]
        is_row = sb("is_row", [P, 3])
        ones_row = sb("ones_row", [3, P], BF16)
        gamma_sb = sb("gamma_sb", [P, D])
        beta_sb = sb("beta_sb", [P, D])
        eps_sb = sb("eps_sb", [P, 1])
        row_i = [sb("src_row_i", [P, HALF, P], I32), sb("dst_row_i", [P, HALF, P], I32)]
        row_f = [sb("src_row_f", [P, HALF, P]), sb("dst_row_f", [P, HALF, P])]
        key = [sb("src_key", [P, HALF * P]), sb("dst_key", [P, HALF * P])]
        safe = [sb("src_safe", [P, tiles], I32), sb("dst_safe", [P, tiles], I32)]
        key_i = sb("key_i", [P, tiles], I32)
        place_i = sb("place_i", [P, 3, tiles], I32)
        place = [sb("src_place", [P, 2, tiles]), sb("dst_place", [P, 2, tiles])]
        dinv = sb("dinv", [P, cols])
        root = sb("root", [P, cols])
        dense = sb("dense", [P, 3 * SLOTS * ROWS, D])
        xin, ain, dout = ([dense[:, (w * SLOTS + k) * ROWS:(w * SLOTS + k + 1) * ROWS, :] for k in range(SLOTS)]
                          for w in range(3))
        self_in = [sb(f"self_in{h}", [P, HALF, D]) for h in range(2)]
        dinv_s = [sb(f"dinv_s{h}", [P, HALF]) for h in range(2)]
        turned = [sb(f"turned{h}", [P, HALF, P]) for h in range(2)]
        stats = [sb(f"stats{h}", [P, ROWS, 6]) for h in range(2)]
        tmp = [sb(f"tmp{h}", [P, 4, ROWS]) for h in range(2)]
        mean = [sb(f"mean{h}", [P, ROWS]) for h in range(2)]
        spread = [sb(f"spread{h}", [P, ROWS]) for h in range(2)]
        dev = [sb(f"dev{h}", [P, ROWS]) for h in range(2)]
        rstd = [sb(f"rstd{h}", [P, ROWS]) for h in range(2)]
        shift = [sb(f"shift{h}", [P, HALF]) for h in range(2)]
        hot_p = [sb(f"hot_p{k}", [P, P], F16) for k in range(HOTS)]
        hot_c = [sb(f"hot_c{k}", [P, cols], F16) for k in range(HOTS)]
        key_s = [sb(f"key_s{g}", [P, HALF]) for g in range(DEEP)]
        take_a = [sb(f"take_a{g}", [P, HALF], I32) for g in range(DEEP)]
        take_b = [sb(f"take_b{g}", [P, HALF], I32) for g in range(DEEP)]
        give = [sb(f"give{g}", [P, HALF], I32) for g in range(2)]
        same = [[sb(f"same{g}_{j}", [P, (j + 2) * P]) for j in range(HALF)] for g in range(2)]
        before = [sb(f"before{g}", [P, HALF]) for g in range(2)]
        to_spare = [sb(f"to_spare{g}", [P, HALF]) for g in range(2)]
        got_a = [[sb(f"got_a{g}_{k}", [P, D]) for k in range(HALF)] for g in range(DEEP)]
        got_b = [[sb(f"got_b{g}_{k}", [P, D]) for k in range(HALF)] for g in range(DEEP)]
        place_s = [sb(f"place_s{g}", [P, HALF]) for g in range(DEEP)]
        hot_t = [sb(f"hot_t{g}", [P, HALF, P]) for g in range(2)]
        weight = [sb(f"weight{g}", [P, HALF]) for g in range(2)]
        ea = [sb(f"ea{g}", [P, HALF, D]) for g in range(2)]
        in_t = [sb(f"in_t{w}", [P, HALF, P]) for w in range(3)]
        hid = [sb(f"hid{g}", [P, HALF, D]) for g in range(2)]
        hid2 = [sb(f"hid2{g}", [P, HALF, D]) for g in range(2)]
        msg = [sb(f"msg{g}", [P, HALF, D]) for g in range(2)]
        total = [sb(f"total{g}", [P, HALF, D]) for g in range(2)]

        bias = [hid[n][0:3, :, :] for n in range(2)]
        bias_part = [buffer[0:3, :, :] for buffer in (hid2[0], hid2[1], msg[0])]
        bias_sum = msg[1][0:3, :, :]

        junk = [buffer[:, :, :].rearrange("p a b -> p (a b)")[:, 0:cols] for buffer in (*in_t, ea[0])]

        bank = [psum(f"bank{k}") for k in range(8)]
        look = [bank[4 + k][:, :, :].rearrange("p a b -> p (a b)")[:, 0:cols] for k in range(HALF)]
        count_ps = bank[0][:, :, :].rearrange("p a b -> p (a b)")[:, 0:cols]

        s_iota, s_const, s_zero, s_weights = sem("s_iota"), sem("s_const"), sem("s_zero"), sem("s_weights")
        s_rows, s_rowf, s_turn_key = sem("s_rows"), sem("s_rowf"), sem("s_turn_key")
        s_bias = sem("s_bias")
        s_dve, s_place = sem("s_dve"), sem("s_place")
        s_issued = sem("s_issued")
        s_hot, s_counted, s_root, s_dinv = sem("s_hot"), sem("s_counted"), sem("s_root"), sem("s_dinv")
        s_fill1, s_fill2 = sem("s_fill1"), sem("s_fill2")
        c_early = sem("c_early")
        c_place, c_hot, c_look, c_pick, c_scaled = (
            sem(n) for n in ("c_place", "c_hot", "c_look", "c_pick", "c_scaled"))
        c_stage, c_got, c_turn, c_same, c_step, c_list, c_sum, c_total, c_put = (
            sem("c_stage"), sems("c_got", DEEP * HALF), sem("c_turn"), sem("c_same"), sem("c_step"), sem("c_list"),
            sem("c_sum"), sem("c_total"), sems("c_put", 2))
        d_sums, d_x, d_st = sems("d_sums", SLOTS), sems("d_xin", SLOTS), sems("d_st", SLOTS)
        d_shift, d_x1_act, d_stage, d_self, d_add, d_scaled, d_turn, d_turned, d_prod, d_pre, d_step, d_stat, d_dev, d_rstd, d_x1 = (
            sem(n) for n in ("d_shift", "d_x1_act", "d_stage", "d_self", "d_add", "d_scaled", "d_turn", "d_turned", "d_prod", "d_pre", "d_step",
                             "d_stat", "d_dev", "d_rstd", "d_x1"))
        e_ea, e_got, e_put = sems("e_ea", 2), sems("e_got", DEEP * HALF), sems("e_put", 2)
        e_stage, e_turn, e_same, e_step, e_list, e_sum, e_total = (
            sem(n) for n in ("e_stage", "e_turn", "e_same", "e_step", "e_list", "e_sum", "e_total"))
        e_in, e_ready, e_h, e_stat, e_mom, e_scaled, e_dev, e_rstd, e_norm, e_msg = (
            sem(n) for n in ("e_in", "e_ready", "e_h", "e_stat", "e_mom", "e_scaled", "e_dev", "e_rstd", "e_norm",
                             "e_msg"))
        f_sums, f_x, f_st = sems("f_sums", SLOTS), sems("f_xin", SLOTS), sems("f_st", SLOTS)
        f_add, f_step, f_stat, f_dev, f_rstd, f_out = (
            sem(n) for n in ("f_add", "f_step", "f_stat", "f_dev", "f_rstd", "f_out"))

        def over(eng, count, period, *parts):
            low, high = min(a for a, _ in parts), max(a for a, _ in parts)

            def step(n):
                for a, part in parts:
                    if 0 <= n + a < count:
                        part((n + a) % period, (n + a) // period)

            first = (period - low + period - 1) // period
            tail_from = (count - 1) // period * period
            last = (tail_from - high) // period
            for n in range(-high, first * period):
                step(n)
            with eng.Fori(first, last) as i:
                for q in range(period):
                    for a, part in parts:
                        part((q + a) % period, i + (q + a) // period)
            for n in range(last * period, count - low):
                step(n)

        def since(eng, semaphore, value):
            if not isinstance(value, int) or value > 0:
                eng.wait_ge(semaphore, value)

        def node_rows(table, c):
            if isinstance(c, int) and c == chunks - 1:
                return table[n_nodes - tail_rows:n_nodes, :].rearrange("(p r) d -> p r d", r=ROWS)
            return table[bass.ds(c * chunk, chunk), :].rearrange("(p r) d -> p r d", r=ROWS)

        def held(c):
            return tail_p if isinstance(c, int) and c == chunks - 1 else P

        def uses(k):
            return len(range(k, chunks, SLOTS))

        groups, units = 2 * rounds, 2 * chunks
        early = len(range(DEEP - 1, groups, DEEP))
        assert early * HALF <= 3 * SLOTS * ROWS

        block = ctx.enter_context(nc.Block())

        @block.sync
        def _(sp):
            sp.wait_ge(s_iota, 2)
            for side, ids in enumerate((dst, src)):
                side = 1 - side
                for c in range(HALF):
                    t0, t1 = c * P, min((c + 1) * P, full_tiles)
                    sp.dma_start(row_i[side][0:t1 - t0, c, :],
                                 ids[t0 * P:t1 * P].rearrange("(t e) -> t e", e=P)).then_inc(s_rows, 16)
                at = full_tiles % P
                sp.dma_start(row_i[side][at:at + 1, HALF - 1, 0:tail_edges],
                             ids[full_tiles * P:n_edges].rearrange("(t e) -> t e", t=1)).then_inc(s_rows, 16)
            for to, of in ((w0_sb[:, :], w0), (w1_sb[:, :, :], w1.rearrange("(w p) d -> p w d", p=P)),
                           *((row[:, j, :], b.rearrange("(a d) -> a d", a=1).to_broadcast([3, D]))
                             for row, b in ((bias[0], b0), (bias[1], b1)) for j in range(HALF))):
                sp.dma_start(to, of).then_inc(s_weights, 16)
            for to, of in ((gamma_sb, gamma), (beta_sb, beta)):
                sp.dma_start(to[:, :], of.rearrange("(a d) -> a d", a=1).to_broadcast([P, D])).then_inc(s_weights, 16)

            def zero_chunk(table, i):
                return sp.dma_start(table[bass.ds(i * chunk, chunk), :].rearrange("(p r) d -> p r d", r=ROWS),
                                    zeros[:, :].rearrange("p (r d) -> p r d", d=D))

            def zero_spare(table):
                return sp.dma_start(table[chunks * chunk:table_rows, :],
                                    zeros[:, 0:(table_rows - chunks * chunk) // P * D])

            sp.wait_ge(s_zero, 1)
            with sp.Fori(0, chunks) as i:
                zero_chunk(agg, i).then_inc(s_fill1, 16)
            zero_spare(agg).then_inc(s_fill1, 16)

            zero_spare(osum).then_inc(s_fill2, 16)
            with sp.Fori(1, chunks + 1) as i:
                sp.wait_ge(c_sum, i * 2 - 1)
                zero_chunk(osum, i - 1).then_inc(s_fill2, 16)

            for s in c_put:
                sp.wait_ge(s, 16 * HALF * rounds)

            def load_d(k, i):
                c = i * SLOTS + k
                since(sp, d_turn, 2 * (c - SLOTS) + 2)
                sp.dma_start(ain[k][0:held(c), :, :], node_rows(agg, c)).then_inc(d_sums[k], 16)
                since(sp, d_x1, 2 * (c - SLOTS) + 2)
                since(sp, d_x1_act, 2 * (c - SLOTS) + 2)
                sp.dma_start(xin[k][0:held(c), :, :], node_rows(x, c)).then_inc(d_x[k], 16)

            over(sp, chunks, SLOTS, (0, load_d))

            def load_e(g, r):
                n = r * 2 + g
                since(sp, e_in, n - 1)
                if isinstance(n, int) and n >= groups - 2:
                    here = min(HALF, full_tiles - n * HALF)
                    if here > 0:
                        sp.dma_start(ea[g][:, 0:here, :], edge_attr[n * HALF * P:(n * HALF + here) * P, :].rearrange(
                            "(k p) d -> p k d", p=P)).then_inc(e_ea[g], 16)
                    if 0 <= here < HALF and tail_edges:
                        sp.dma_start(ea[g][0:tail_edges, here, :],
                                     edge_attr[full_tiles * P:n_edges, :]).then_inc(e_ea[g], 16)
                else:
                    sp.dma_start(ea[g][:, :, :], edge_attr[bass.ds(n * HALF * P, HALF * P), :].rearrange(
                        "(k p) d -> p k d", p=P)).then_inc(e_ea[g], 16)

            over(sp, groups, 2, (0, load_e))

            for s in e_put:
                sp.wait_ge(s, 16 * HALF * rounds)

            def load_f(k, i):
                c = i * SLOTS + k
                since(sp, f_add, c - SLOTS + 1)
                sp.dma_start(ain[k][0:held(c), :, :], node_rows(osum, c)).then_inc(f_sums[k], 16)
                since(sp, f_out, c - SLOTS + 1)
                sp.dma_start(xin[k][0:held(c), :, :], node_rows(x1_dram, c)).then_inc(f_x[k], 16)

            over(sp, chunks, SLOTS, (0, load_f))

            for k in range(SLOTS):
                sp.wait_ge(f_st[k], 16 * uses(k))

        @block.gpsimd
        def _(pool):
            for side in range(2):
                nc.gpsimd.iota(row_i[side][:, HALF - 1, :], pattern=[[1, P]], base=spare,
                               channel_multiplier=0).then_inc(s_iota, 1)
            nc.gpsimd.iota(iota_i[:, :], pattern=[[1, cols]], base=0, channel_multiplier=0).then_inc(s_iota, 1)
            nc.gpsimd.iota(spare_i[:, :], pattern=[[P, HALF]], base=spare + P, channel_multiplier=1).then_inc(s_iota, 1)
            nc.gpsimd.iota(own_i[:, :], pattern=[[1, 1]], base=0, channel_multiplier=1).then_inc(s_iota, 1)
            nc.gpsimd.memset(ident[:, :], 0.0).then_inc(s_const, 1)
            nc.gpsimd.memset(earlier[:, :], 1.0).then_inc(s_const, 1)
            nc.gpsimd.memset(eps_sb[:, :], EPS).then_inc(s_const, 1)
            nc.gpsimd.memset(ones_row[:, :], 1.0).then_inc(s_const, 1)
            pool.wait_ge(s_const, 4)
            nc.gpsimd.affine_select(out=ident[:, :], in_=ident[:, :], compare_op=ALU.not_equal, fill=1.0, base=0,
                                    pattern=[[-1, P]], channel_multiplier=1).then_inc(s_const, 1)
            nc.gpsimd.affine_select(out=earlier[:, (HALF - 1) * P:HALF * P],
                                    in_=earlier[:, (HALF - 1) * P:HALF * P], compare_op=ALU.is_gt, fill=0.0, base=0,
                                    pattern=[[-1, P]], channel_multiplier=1).then_inc(s_const, 1)
            nc.gpsimd.memset(zeros[:, :], 0.0).then_inc(s_zero, 1)

            def take(table, lists, staged, into, got, used, k):
                def part(g, r):
                    n = r * DEEP + g
                    if staged is not None and k == 0:
                        since(pool, used, n - DEEP + 1)
                        pool.wait_ge(staged, n + 1)
                        pool.sem_inc(s_issued, 1)
                    nc.gpsimd.indirect_dma_start(
                        into[g][k][:, :], None, table, bass.IndirectOffsetOnAxis(lists[g][:, k:k + 1], 0),
                        bounds_check=n_nodes - 1, oob_is_err=True).then_inc(got[g * HALF + k], 16)
                return part

            def put(table, listed, copied, added, k):
                def part(g, r):
                    n, r, g = r * DEEP + g, r * (DEEP // 2) + g // 2, g % 2
                    if k == 0:
                        pool.wait_ge(listed, n + 1)
                        pool.wait_ge(copied, n + 1)
                        since(pool, added[1 - g], (r + g) * HALF * 16)
                        pool.sem_inc(s_issued, 1)
                    nc.gpsimd.indirect_dma_start(
                        table, bass.IndirectOffsetOnAxis(give[g][:, k:k + 1], 0), total[g][:, k, :], None,
                        bounds_check=table_rows - 1, oob_is_err=True, compute_op=ALU.add).then_inc(added[g], 16)
                return part

            def first_put(g, r):
                if isinstance(r, int) and r == 0 and g == 0:
                    pool.wait_ge(s_fill1, 16 * (chunks + 1))
                put(agg, c_list, c_total, c_put, 0)(g, r)

            def take_c(k):
                def part(g, r):
                    if g < DEEP - 1:
                        take(x, take_a, c_stage, got_a, c_got, c_scaled, k)(g, r)
                return part

            for g in range(DEEP - 1):
                for k in range(HALF):
                    take_c(k)(g, 0)
            for r in range(early):
                for k in range(HALF):
                    t = (r * DEEP + DEEP - 1) * HALF + k
                    nc.gpsimd.indirect_dma_start(
                        dense[:, r * HALF + k, :], None, x, bass.IndirectOffsetOnAxis(safe[0][:, t:t + 1], 0),
                        bounds_check=n_nodes - 1, oob_is_err=True).then_inc(c_early, 16)

            def take_rest(k):
                def part(g, r):
                    if not isinstance(r, int) or r > 0:
                        take_c(k)(g, r)
                return part

            over(pool, groups, DEEP, (0, first_put), *((0, put(agg, c_list, c_total, c_put, k)) for k in range(1, HALF)),
                 *((3, take_rest(k)) for k in range(HALF)))

            def add_d(q, i):
                k, h, u = q // 2, q % 2, i * 2 * SLOTS + q
                part = slice(h * HALF, (h + 1) * HALF)
                pool.wait_ge(d_stage, u + 1)
                since(pool, d_add, u - 1)
                nc.gpsimd.tensor_tensor(self_in[h][:, :, :], xin[k][:, part, :],
                                        dinv_s[h][:, :].unsqueeze(2).to_broadcast([P, HALF, D]),
                                        ALU.mult).then_inc(d_self, 1)
                if h == 0:
                    pool.wait_ge(d_sums[k], i * 16 + 16)
                pool.wait_ge(d_self, u + 1)
                nc.gpsimd.tensor_tensor(ain[k][:, part, :], ain[k][:, part, :], self_in[h][:, :, :],
                                        ALU.add).then_inc(d_add, 1)

            over(pool, units, 2 * SLOTS, (0, add_d))

            for k in range(SLOTS):
                pool.wait_ge(d_st[k], 16 * uses(k))
            pool.wait_ge(s_fill2, 16 * (chunks + 1))
            parts = []
            for k in range(HALF):
                parts.append((-1, put(osum, e_list, e_total, e_put, k)))
            for k in range(HALF):
                parts.append((3, take(x1_dram, take_a, e_stage, got_a, e_got, e_in, k)))
                parts.append((3, take(x1_dram, take_b, None, got_b, e_got, e_in, k)))
            over(pool, groups, DEEP, *parts)

            def add_f(k, i):
                pool.wait_ge(f_sums[k], i * 16 + 16)
                pool.wait_ge(f_x[k], i * 16 + 16)
                nc.gpsimd.tensor_tensor(xin[k][:, :, :], ain[k][:, :, :], xin[k][:, :, :], ALU.add).then_inc(f_add, 1)

            over(pool, chunks, SLOTS, (0, add_f))

        @block.tensor
        def _(pe):
            pe.wait_ge(s_const, 6)
            pe.wait_ge(s_rowf, 2)
            for side in range(2):
                for c in range(HALF):
                    n = min(P, tiles - c * P)
                    last = nc.tensor.transpose(bank[1 + side][:, c, 0:n], row_f[side][0:n, c, :], ident[0:n, 0:n])
                last.then_inc(s_turn_key, 1)

            def count(k, i):
                t = i * HOTS + k
                pe.wait_ge(s_hot, t + 1)
                nc.tensor.matmul(count_ps, hot_p[k][:, :], hot_c[k][:, :], start=isinstance(t, int) and t == 0,
                                 stop=isinstance(t, int) and t == tiles - 1).then_inc(s_counted, 1)

            over(pe, tiles, HOTS, (0, count))

            def turn_keys(staged, compared, turn):
                def part(g, r):
                    n = r * DEEP + g
                    pe.wait_ge(staged, n + 1)
                    since(pe, compared, n - 1)
                    for k in range(HALF):
                        last = nc.tensor.transpose(bank[g % 2][:, k, :], key_s[g][:, k:k + 1].to_broadcast([P, P]),
                                                   ident[:, :])
                    last.then_inc(turn, 1)
                return part

            def sum_group(of, g, h, place_of):
                for t in range(HALF):
                    for j in range(t, HALF):
                        at = (j + 1) * P if j == t else t * P
                        last = nc.tensor.matmul(place_of[:, t, :], same[h][j][:, at:at + P], of[h][:, j, :],
                                                start=j == t, stop=j == HALF - 1)
                return last

            pe.wait_ge(s_root, 1)
            pe.wait_ge(s_dinv, 1)

            def turn_place(g, r):
                n = r * DEEP + g
                pe.wait_ge(c_stage, n + 1)
                since(pe, c_hot, n)
                for k in range(HALF):
                    last = nc.tensor.transpose(bank[2][:, k, :], place_s[g][:, k:k + 1].to_broadcast([P, P]),
                                               ident[:, :])
                last.then_inc(c_place, 1)

            def look_up(g, r):
                n = r * DEEP + g
                pe.wait_ge(c_hot, n + 1)
                since(pe, c_pick, n)
                for k in range(HALF):
                    last = nc.tensor.matmul(look[k], hot_t[g % 2][:, k, :], dinv[:, :], start=True, stop=True)
                last.then_inc(c_look, 1)

            def sum_c(g, r):
                n = r * DEEP + g
                pe.wait_ge(c_same, n + 1)
                pe.wait_ge(c_scaled, n + 1)
                since(pe, c_total, n)
                sum_group(hid, g, g % 2, bank[3]).then_inc(c_sum, 1)

            over(pe, groups, DEEP, (2, look_up), (3, turn_place), (0, sum_c), (3, turn_keys(c_stage, c_same, c_turn)))

            pe.wait_ge(s_weights, (4 + 2 * HALF) * 16)
            pe.wait_ge(s_bias, 2)
            pe.wait_ge(c_same, groups)
            pe.wait_ge(c_total, groups)

            def turn_d(q, i):
                k, h, u = q // 2, q % 2, i * 2 * SLOTS + q
                pe.wait_ge(d_scaled, u + 1)
                since(pe, d_turned, u - 1)
                for j in range(HALF):
                    last = nc.tensor.transpose(bank[h][:, j, :], ain[k][:, h * HALF + j, :], ident[:, :])
                last.then_inc(d_turn, 1)

            def prod_d(q, i):
                h, u = q % 2, i * 2 * SLOTS + q
                pe.wait_ge(d_turned, u + 1)
                since(pe, d_pre, u - 1)
                for j in range(HALF):
                    nc.tensor.matmul(bank[2 + h][:, j, :], turned[h][:, j, :], w0_sb[:, :], start=j == 0, stop=False,
                                     skip_group_check=True)
                nc.tensor.matmul(bank[2 + h][:, :, :], ones_row[:, :], bias_row[0][:, :, :], start=False, stop=True,
                                 skip_group_check=True).then_inc(d_prod, 1)

            over(pe, units, 2 * SLOTS, (2, turn_d), (1, prod_d))

            pe.wait_ge(d_pre, units)

            def turn_in(g, r):
                n, v, h = r * DEEP + g, r * (DEEP // 2) + g // 2, g % 2
                since(pe, e_ready, n)
                for w, rows in enumerate((got_a, got_b)):
                    for k in range(HALF):
                        pe.wait_ge(e_got[g * HALF + k], r * 32 + 32)
                        nc.tensor.transpose(bank[4 + w][:, k, :], rows[g][k][:, :], ident[:, :])
                loads = 1
                if isinstance(n, int) and n >= groups - 2:
                    here = full_tiles - n * HALF
                    loads = (1 if here > 0 else 0) + (1 if 0 <= here < HALF and tail_edges else 0)
                pe.wait_ge(e_ea[h], v * 16 + loads * 16)
                for k in range(HALF):
                    last = nc.tensor.transpose(bank[6][:, k, :], ea[h][:, k, :], ident[:, :])
                last.then_inc(e_in, 1)

            def hidden(g, r):
                n = r * DEEP + g
                pe.wait_ge(e_ready, n + 1)
                since(pe, e_scaled, n)
                for k in range(HALF):
                    for w in range(3):
                        nc.tensor.matmul(bank[7][:, k, :], in_t[w][:, k, :], w1_sb[:, w, :],
                                         start=k == 0 and w == 0, stop=False, skip_group_check=True)
                last = nc.tensor.matmul(bank[7][:, :, :], ones_row[:, :], bias_row[1][:, :, :], start=False, stop=True,
                                        skip_group_check=True)
                last.then_inc(e_h, 1)

            def sum_e(g, r):
                n, g = r * DEEP + g, g % 2
                pe.wait_ge(e_msg, n + 1)
                since(pe, e_total, n - 1)
                sum_group(msg, g, g, bank[2 + g]).then_inc(e_sum, 1)

            over(pe, groups, DEEP, (1, hidden), (0, sum_e), (2, turn_keys(e_stage, e_same, e_turn)), (2, turn_in))

        @block.scalar
        def _(act):
            act.wait_ge(s_counted, tiles)
            nc.scalar.activation(root[:, :], count_ps, ACT.Sqrt, bias=1.0).then_inc(s_root, 1)

            def copy_sums(summed, added, copied, banks):
                def part(g, r):
                    g, r = g % 2, r * (DEEP // 2) + g // 2
                    act.wait_ge(summed, r * 2 + g + 1)
                    since(act, added[g], r * HALF * 16)
                    nc.scalar.copy(total[g][:, :, :], banks[g][:, :, :]).then_inc(copied, 1)
                return part

            def scale_c(g, r):
                n, h = r * DEEP + g, g % 2
                act.wait_ge(c_pick, n + 1)
                since(act, c_sum, n - 1)
                for k in range(HALF):
                    if g < DEEP - 1:
                        act.wait_ge(c_got[g * HALF + k], r * 16 + 16)
                        rows = got_a[g][k][:, :]
                    else:
                        rows = dense[:, bass.ds(r * HALF + k, 1), :].rearrange("p a b -> p (a b)")
                    last = nc.scalar.activation(hid[h][:, k, :], rows, ACT.Copy,
                                                scale=weight[h][:, k:k + 1])
                last.then_inc(c_scaled, 1)

            act.wait_ge(c_early, 16 * early * HALF)
            over(act, groups, DEEP, (1, scale_c), (0, copy_sums(c_sum, c_put, c_total, (bank[3], bank[3]))))

            def scale_d(q, i):
                k, h, u = q // 2, q % 2, i * 2 * SLOTS + q
                act.wait_ge(d_add, u + 1)
                for j in range(HALF):
                    rows = ain[k][:, h * HALF + j, :]
                    last = nc.scalar.activation(rows, rows, ACT.Copy, scale=dinv[:, bass.ds(u * HALF + j, 1)])
                last.then_inc(d_scaled, 1)

            def turned_d(q, i):
                h, u = q % 2, i * 2 * SLOTS + q
                act.wait_ge(d_turn, u + 1)
                since(act, d_prod, u - 1)
                nc.scalar.copy(turned[h][:, :, :], bank[h][:, :, :]).then_inc(d_turned, 1)

            def dev_d(q, i):
                h, u = q % 2, i * 2 * SLOTS + q
                act.wait_ge(d_stat, u + 1)
                since(act, d_rstd, u - 1)
                nc.scalar.activation(dev[h][:, 0:HALF], spread[h][:, 0:HALF], ACT.Sqrt, bias=eps_sb[:, :],
                                     scale=1.0 / D).then_inc(d_dev, 1)

            def normal_act(q, i):
                k, h, u = q // 2, q % 2, i * 2 * SLOTS + q
                act.wait_ge(d_shift, u + 1)
                if h == 0:
                    since(act, d_st[k], i * 16)
                for j in range(BY_ACT):
                    last = nc.scalar.activation(dout[k][:, h * HALF + j, :], xin[k][:, h * HALF + j, :], ACT.Identity,
                                                bias=shift[h][:, j:j + 1], scale=rstd[h][:, j:j + 1])
                last.then_inc(d_x1_act, 1)

            def store_d(q, i):
                k, h, c = q // 2, q % 2, i * SLOTS + q // 2
                if h == 1:
                    act.wait_ge(d_x1_act, i * 2 * SLOTS + q + 1)
                    act.wait_ge(d_x1, i * 2 * SLOTS + q + 1)
                    act.dma_start(node_rows(x1_dram, c), dout[k][0:held(c), :, :]).then_inc(d_st[k], 16)

            over(act, units, 2 * SLOTS, (3, scale_d), (2, turned_d), (-1, normal_act), (0, dev_d), (-2, store_d))

            def ready(g, r):
                n = r * DEEP + g
                act.wait_ge(e_in, n + 1)
                since(act, e_h, n)
                for w in range(3):
                    last = nc.scalar.copy(in_t[w][:, :, :], bank[4 + w][:, :, :])
                last.then_inc(e_ready, 1)

            def dev_e(g, r):
                n, g = r * DEEP + g, g % 2
                act.wait_ge(e_stat, n + 1)
                since(act, e_rstd, n - 1)
                nc.scalar.activation(dev[g][:, 0:HALF], spread[g][:, 0:HALF], ACT.Sqrt, bias=eps_sb[:, :],
                                     scale=1.0 / D).then_inc(e_dev, 1)

            def messages(g, r):
                n, g = r * DEEP + g, g % 2
                act.wait_ge(e_norm, n + 1)
                since(act, e_sum, n - 1)
                nc.scalar.activation(msg[g][:, :, :], hid2[g][:, :, :], ACT.Relu).then_inc(e_msg, 1)

            over(act, groups, DEEP, (0, dev_e), (0, messages),
                 (0, copy_sums(e_sum, e_put, e_total, (bank[2], bank[3]))), (2, ready))

            def dev_f(k, i):
                c = i * SLOTS + k
                act.wait_ge(f_stat, c + 1)
                since(act, f_rstd, c - 1)
                nc.scalar.activation(dev[k % 2][:, :], spread[k % 2][:, :], ACT.Sqrt, bias=eps_sb[:, :],
                                     scale=1.0 / D).then_inc(f_dev, 1)

            def store_f(k, i):
                c = i * SLOTS + k
                act.wait_ge(f_out, c + 1)
                act.dma_start(node_rows(out, c), dout[k][0:held(c), :, :]).then_inc(f_st[k], 16)

            over(act, chunks, SLOTS, (1, dev_f), (0, store_f))

        @block.vector
        def _(dve):
            made = [0]

            def link(ins):
                made[0] += 1
                ins.then_inc(s_dve, 1)
                dve.wait_ge(s_dve, made[0])

            dve.wait_ge(s_iota, 5)
            nc.vector.tensor_copy(iota_h[:, :], iota_i[:, :])
            nc.vector.tensor_copy(own_f[:, :], own_i[:, :])
            link(nc.vector.tensor_copy(spare_f[:, :], spare_i[:, :]))
            dve.wait_ge(s_rows, 16 * 2 * (HALF + 1))
            for side in range(2):
                nc.vector.tensor_copy(row_f[side][:, 0:HALF - 1, :], row_i[side][:, 0:HALF - 1, :])
                n = tiles - (HALF - 1) * P
                nc.vector.tensor_copy(row_f[side][0:n, HALF - 1, :],
                                      row_i[side][0:n, HALF - 1, :]).then_inc(s_rowf, 1)
            for side in range(2):
                dve.wait_ge(s_turn_key, side + 1)
                link(nc.vector.tensor_copy(key[side][:, 0:tiles],
                                           bank[1 + side][:, :, :].rearrange("p a b -> p (a b)")[:, 0:tiles]))
                link(nc.vector.tensor_scalar(safe[side][:, :], key[side][:, 0:tiles], float(n_nodes - 1), None,
                                             ALU.min))
            for side in range(2):
                link(nc.vector.tensor_copy(key_i[:, :], key[side][:, 0:tiles]))
                nc.vector.tensor_scalar(place_i[:, 0, :], key_i[:, :], LOG_ROWS, P - 1, ALU.arith_shift_right,
                                        ALU.bitwise_and)
                nc.vector.tensor_scalar(place_i[:, 1, :], key_i[:, :], LOG_CHUNK, None, ALU.arith_shift_right)
                link(nc.vector.tensor_scalar(place_i[:, 2, :], key_i[:, :], ROWS - 1, None, ALU.bitwise_and))
                nc.vector.tensor_copy(place[side][:, 0, :], place_i[:, 0, :])
                link(nc.vector.scalar_tensor_tensor(out=place[side][:, 1, :], in0=place_i[:, 1, :],
                                                    scalar=float(ROWS), in1=place_i[:, 2, :], op0=ALU.mult,
                                                    op1=ALU.add))

            def stage(key_side, lists, got, uses, compared, staged, listed=DEEP):
                def part(g, r):
                    n = r * DEEP + g
                    since(dve, compared, n - DEEP + 1)
                    for side, to in lists if g < listed else ():
                        for k in range(HALF):
                            since(dve, got[g * HALF + k], r * uses * 16)
                        nc.vector.tensor_copy(to[g][:, :], safe[side][:, bass.ds(n * HALF, HALF)])
                    if key_side == 1:
                        nc.vector.tensor_copy(place_s[g][:, :], place[0][:, 0, bass.ds(n * HALF, HALF)])
                    nc.vector.tensor_copy(key_s[g][:, :], key[key_side][:, bass.ds(n * HALF, HALF)]).then_inc(
                        staged, 1)
                return part

            dve.wait_ge(s_weights, (4 + 2 * HALF) * 16)
            for m in range(3):
                last = nc.vector.tensor_scalar(is_row[:, m:m + 1], own_f[:, :], float(m), None, ALU.is_equal)
            link(last)
            for b in range(2):
                rest = bias[b]
                for m in range(2):
                    link(nc.vector.tensor_copy(bias_hi[:, :, :], rest))
                    link(nc.vector.tensor_copy(bias_part[m], bias_hi[:, :, :]))
                    to = bias_part[2] if m == 1 else bias_sum
                    link(nc.vector.tensor_tensor(to, rest, bias_part[m], ALU.subtract))
                    rest = to
                link(nc.vector.tensor_scalar(bias_sum, bias_part[0], is_row[0:3, 0:1], None, ALU.mult))
                for m in (1, 2):
                    link(nc.vector.scalar_tensor_tensor(
                        out=bias_sum, in0=bias_part[m], scalar=is_row[0:3, m:m + 1], in1=bias_sum,
                        op0=ALU.mult, op1=ALU.add))
                nc.vector.tensor_copy(bias_row[b][:, :, :], bias_sum).then_inc(s_bias, 1)
                dve.wait_ge(s_bias, b + 1)

            stage_c = stage(1, ((0, take_a),), c_got, 1, c_same, c_stage, DEEP - 1)
            for g in range(DEEP):
                stage_c(g, 0)

            def one_hot(k, i):
                t = i * HOTS + k
                if k % 4 == 0:
                    since(dve, s_counted, t - HOTS + 4)
                nc.vector.tensor_scalar(hot_p[k][:, :], iota_h[:, 0:P], place[1][:, 0, bass.ds(t, 1)], None,
                                        ALU.is_equal)
                nc.vector.tensor_scalar(hot_c[k][:, :], iota_h[:, :], place[1][:, 1, bass.ds(t, 1)], None,
                                        ALU.is_equal).then_inc(s_hot, 1)

            over(dve, tiles, HOTS, (0, one_hot))

            dve.wait_ge(s_root, 1)
            nc.vector.reciprocal(dinv[:, :], root[:, :]).then_inc(s_dinv, 1)
            dve.wait_ge(s_dinv, 1)

            def compare(turn, summed, compared):
                def part(g, r):
                    n, h = r * DEEP + g, g % 2
                    dve.wait_ge(turn, n + 1)
                    since(dve, summed, n - 1)
                    row = bank[h][:, :, :].rearrange("p a b -> p (a b)")
                    for j in range(HALF):
                        nc.vector.scalar_tensor_tensor(
                            out=same[h][j][:, 0:(j + 1) * P], in0=row[:, 0:(j + 1) * P], scalar=key_s[g][:, j:j + 1],
                            in1=earlier[:, (HALF - 1 - j) * P:HALF * P], op0=ALU.is_equal, op1=ALU.mult,
                            accum_out=before[h][:, j:j + 1])
                        last = nc.vector.tensor_scalar(same[h][j][:, (j + 1) * P:(j + 2) * P],
                                                       row[:, j * P:(j + 1) * P], key_s[g][:, j:j + 1], None,
                                                       ALU.is_equal)
                    last.then_inc(compared, 1)
                return part

            def rows_to_add(key_side, compared, stepped, added, listed):
                def part(g, r):
                    n, r, g = r * DEEP + g, r * (DEEP // 2) + g // 2, g % 2
                    keys = key[key_side][:, bass.ds(n * HALF, HALF)]
                    dve.wait_ge(compared, n + 1)
                    nc.vector.tensor_scalar(before[g][:, :], before[g][:, :], 1.0, None, ALU.min)
                    nc.vector.tensor_tensor(to_spare[g][:, :], spare_f[:, :], keys,
                                            ALU.subtract).then_inc(stepped, 1)
                    dve.wait_ge(stepped, n * 2 + 1)
                    nc.vector.tensor_tensor(to_spare[g][:, :], to_spare[g][:, :], before[g][:, :],
                                            ALU.mult).then_inc(stepped, 1)
                    dve.wait_ge(stepped, n * 2 + 2)
                    since(dve, added[g], r * HALF * 16)
                    nc.vector.tensor_tensor(give[g][:, :], to_spare[g][:, :], keys,
                                            ALU.add).then_inc(listed, 1)
                return part

            def moments(h, n, step, done, at, finished):
                m0, v0, m1, v1 = (stats[h][:, 0:n, c] for c in (1, 2, 4, 5))
                dve.wait_ge(done, at + step + 1)
                if step == 0:
                    nc.vector.tensor_tensor(tmp[h][:, 0, 0:n], m0, m1, ALU.add)
                    nc.vector.tensor_tensor(tmp[h][:, 1, 0:n], m0, m1, ALU.subtract)
                    nc.vector.tensor_tensor(tmp[h][:, 2, 0:n], v0, v1, ALU.add).then_inc(done, 1)
                elif step == 1:
                    nc.vector.tensor_scalar(mean[h][:, 0:n], tmp[h][:, 0, 0:n], 0.5, None, ALU.mult)
                    nc.vector.tensor_tensor(tmp[h][:, 3, 0:n], tmp[h][:, 1, 0:n], tmp[h][:, 1, 0:n],
                                            ALU.mult).then_inc(done, 1)
                else:
                    nc.vector.scalar_tensor_tensor(out=spread[h][:, 0:n], in0=tmp[h][:, 3, 0:n], scalar=D / 4.0,
                                                   in1=tmp[h][:, 2, 0:n], op0=ALU.mult,
                                                   op1=ALU.add).then_inc(finished, 1)

            def hot_places(g, r):
                n, h = r * DEEP + g, g % 2
                dve.wait_ge(c_place, n + 1)
                since(dve, c_look, n - 1)
                nc.vector.tensor_scalar(hot_t[h][:, :, :], bank[2][:, :, :], own_f[:, 0:1], None,
                                        ALU.is_equal).then_inc(c_hot, 1)

            def pick(g, r):
                n, h = r * DEEP + g, g % 2
                dve.wait_ge(c_look, n + 1)
                since(dve, c_scaled, n - 1)
                for k in range(HALF):
                    last = nc.vector.scalar_tensor_tensor(
                        out=junk[k], in0=iota_h[:, :], scalar=place[0][:, 1, bass.ds(n * HALF + k, 1)],
                        in1=look[k], op0=ALU.is_equal, op1=ALU.mult, accum_out=weight[h][:, k:k + 1])
                last.then_inc(c_pick, 1)

            def stage_rest(g, r):
                if not isinstance(r, int) or r > 0:
                    stage_c(g, r)

            over(dve, groups, DEEP, (1, pick), (2, hot_places), (1, compare(c_turn, c_sum, c_same)),
                 (0, rows_to_add(1, c_same, c_step, c_put, c_list)), (4, stage_rest))

            def residual(q, i):
                k, h, u = q // 2, q % 2, i * 2 * SLOTS + q
                part = slice(h * HALF, (h + 1) * HALF)
                since(dve, d_self, u + 1)
                dve.wait_ge(d_prod, u + 1)
                nc.vector.scalar_tensor_tensor(
                    out=xin[k][:, part, :], in0=bank[2 + h][:, :, :], scalar=0.0, in1=xin[k][:, part, :], op0=ALU.max,
                    op1=ALU.add).then_inc(d_pre, 1)

            def stats_d(q, i):
                k, h, u = q // 2, q % 2, i * 2 * SLOTS + q
                dve.wait_ge(d_pre, u + 1)
                for j in range(HALF):
                    last = nc.vector.bn_stats(stats[h][:, j, :], xin[k][:, h * HALF + j, :])
                last.then_inc(d_step, 1)

            def rstd_d(q, i):
                h, u = q % 2, i * 2 * SLOTS + q
                dve.wait_ge(d_dev, u + 1)
                since(dve, d_x1_act, u - 1)
                nc.vector.reciprocal(rstd[h][:, 0:HALF], dev[h][:, 0:HALF]).then_inc(d_rstd, 1)

            def shift_d(q, i):
                h, u = q % 2, i * 2 * SLOTS + q
                dve.wait_ge(d_rstd, u + 1)
                nc.vector.scalar_tensor_tensor(out=shift[h][:, :], in0=mean[h][:, 0:HALF], scalar=-1.0,
                                               in1=rstd[h][:, 0:HALF], op0=ALU.mult, op1=ALU.mult).then_inc(d_shift, 1)

            def normal_d(j):
                def part(q, i):
                    k, h, u = q // 2, q % 2, i * 2 * SLOTS + q
                    if j == BY_ACT and h == 0:
                        since(dve, d_st[k], i * 16)
                    done = nc.vector.tensor_scalar(dout[k][:, h * HALF + j, :], xin[k][:, h * HALF + j, :],
                                                   mean[h][:, j:j + 1], rstd[h][:, j:j + 1], ALU.subtract, ALU.mult)
                    if j == HALF - 1:
                        done.then_inc(d_x1, 1)
                return part

            def stage_d(q, i):
                k, h, u = q // 2, q % 2, i * 2 * SLOTS + q
                dve.wait_ge(d_x[k], i * 16 + 16)
                since(dve, d_self, u - 1)
                nc.vector.tensor_copy(dinv_s[h][:, :], dinv[:, bass.ds(u * HALF, HALF)]).then_inc(d_stage, 1)

            def moments_d(step):
                def part(q, i):
                    moments(q % 2, HALF, step, d_step, (i * 2 * SLOTS + q) * 3, d_stat)
                return part

            over(dve, units, 2 * SLOTS, (4, stage_d), (0, residual), (-1, rstd_d), (0, stats_d), (-1, shift_d),
                 (0, moments_d(0)), (-1, normal_d(2)), (0, moments_d(1)), (-1, normal_d(3)), (0, moments_d(2)))

            def normal_e(g, r):
                n, g = r * DEEP + g, g % 2
                dve.wait_ge(e_h, n + 1)
                for k in range(HALF):
                    last = nc.vector.bn_stats(stats[g][:, k, :], bank[7][:, k, :])
                last.then_inc(e_mom, 1)
                for step in range(3):
                    moments(g, HALF, step, e_mom, n * 3, e_stat)
                dve.wait_ge(e_stat, n + 1)
                for k in range(HALF):
                    last = nc.vector.scalar_tensor_tensor(
                        out=hid[g][:, k, :], in0=bank[7][:, k, :], scalar=mean[g][:, k:k + 1], in1=gamma_sb[:, :],
                        op0=ALU.subtract, op1=ALU.mult)
                last.then_inc(e_scaled, 1)
                dve.wait_ge(e_dev, n + 1)
                nc.vector.reciprocal(rstd[g][:, 0:HALF], dev[g][:, 0:HALF]).then_inc(e_rstd, 1)
                dve.wait_ge(e_rstd, n + 1)
                dve.wait_ge(e_scaled, n + 1)
                since(dve, e_msg, n - 1)
                for k in range(HALF):
                    last = nc.vector.scalar_tensor_tensor(
                        out=hid2[g][:, k, :], in0=hid[g][:, k, :], scalar=rstd[g][:, k:k + 1], in1=beta_sb[:, :],
                        op0=ALU.mult, op1=ALU.add)
                last.then_inc(e_norm, 1)

            over(dve, groups, DEEP, (0, normal_e), (0, rows_to_add(0, e_same, e_step, e_put, e_list)),
                 (1, compare(e_turn, e_sum, e_same)),
                 (4, stage(0, ((0, take_a), (1, take_b)), e_got, 2, e_same, e_stage)))

            def stats_f(k, i):
                c = i * SLOTS + k
                dve.wait_ge(f_add, c + 1)
                for j in range(ROWS):
                    last = nc.vector.bn_stats(stats[k % 2][:, j, :], xin[k][:, j, :])
                last.then_inc(f_step, 1)

            def moments_f(step):
                def part(k, i):
                    moments(k % 2, ROWS, step, f_step, (i * SLOTS + k) * 3, f_stat)
                return part

            def rstd_f(k, i):
                dve.wait_ge(f_dev, i * SLOTS + k + 1)
                nc.vector.reciprocal(rstd[k % 2][:, :], dev[k % 2][:, :]).then_inc(f_rstd, 1)

            def normal_f(js):
                def part(k, i):
                    if js[0] == 0:
                        dve.wait_ge(f_rstd, i * SLOTS + k + 1)
                        since(dve, f_st[k], i * 16)
                    for j in js:
                        last = nc.vector.tensor_scalar(dout[k][:, j, :], xin[k][:, j, :], mean[k % 2][:, j:j + 1],
                                                       rstd[k % 2][:, j:j + 1], ALU.subtract, ALU.mult)
                    if js[-1] == ROWS - 1:
                        last.then_inc(f_out, 1)
                return part

            over(dve, chunks, SLOTS, (0, rstd_f), (1, stats_f), (0, normal_f((0, 1))), (1, moments_f(0)),
                 (0, normal_f((2, 3))), (1, moments_f(1)), (0, normal_f((4, 5))), (1, moments_f(2)),
                 (0, normal_f((6, 7))))


_INS = ["x", "src", "dst", "edge_attr_128", "L0_gnn_W", "L0_gnn_b", "L1_gnn_W", "L1_gnn_b", "L1_gnn_gamma",
        "L1_gnn_beta"]


def kernel(**inputs):
    import numpy as np
    import concourse.bacc as bacc
    from concourse import mybir as _mybir
    from concourse.bass_utils import run_bass_kernel_spmd

    nc = bacc.Bacc("TRN2", target_bir_lowering=False, num_devices=1)
    arrays, args = {}, []
    for name in _INS:
        a = np.ascontiguousarray(inputs[name])
        arrays[f"in_{name}"] = a
        args.append(nc.dram_tensor(f"in_{name}", a.shape, _mybir.dt.from_np(a.dtype), kind="ExternalInput").ap())
    result = nc.dram_tensor("out_x", inputs["x"].shape, _mybir.dt.float32, kind="ExternalOutput").ap()
    program(nc, *args, result)
    r = run_bass_kernel_spmd(nc, [arrays], core_ids=[0])
    return r.results[0]["out_x"]
```

```python
from contextlib import ExitStack

import concourse.bass as bass
from concourse import mybir

F32 = mybir.dt.float32
F16 = mybir.dt.float16
BF16 = mybir.dt.bfloat16
I32 = mybir.dt.int32
ALU = mybir.AluOpType
ACT = mybir.ActivationFunctionType

P = 128
EPS = 1e-5
ROWS = 8
HALF = 4
SLOTS = 6
HOTS = 8
HOTS_ACT = (0, 2, 4, 5, 7)
DEEP = 4
ACT_BLOCKS = ((0, 1), (4,))
DVE_BLOCKS = ((2, 3), (5, 6, 7))
ACT_LAST = 2
LOG_ROWS = 3
LOG_CHUNK = 10


def program(nc, x, src, dst, edge_attr, w0, b0, w1, b1, gamma, beta, out):
    n_nodes, D = x.shape
    n_edges = src.shape[0]
    chunk = P * ROWS
    chunks = -(-n_nodes // chunk)
    cols = chunks * ROWS
    tail_rows = n_nodes - (chunks - 1) * chunk
    tail_p = tail_rows // ROWS
    assert tail_p * ROWS == tail_rows and chunks % 2 == 1
    spare = -(-n_nodes // P) * P
    table_rows = spare + (1 + HALF) * P
    tiles = -(-n_edges // (2 * HALF * P)) * 2 * HALF
    rounds = tiles // (2 * HALF)
    full_tiles, tail_edges = divmod(n_edges, P)
    assert D == P and cols * P == spare + P and cols <= 512

    def dram(name, rows=table_rows):
        return nc.dram_tensor(name, (rows, D), F32, kind="Internal").ap()

    x1_dram = dram("x1_dram", n_nodes)
    agg, osum = dram("agg"), dram("osum")

    with ExitStack() as ctx:
        def sb(name, shape, dt=F32):
            return ctx.enter_context(nc.sbuf_tensor(name, shape, dt))

        def psum(name, shape=(P, HALF, P)):
            return ctx.enter_context(nc.psum_tensor(name, list(shape), F32))

        def sem(name):
            return ctx.enter_context(nc.semaphore(name))

        def sems(name, n):
            return [sem(f"{name}{k}") for k in range(n)]

        ident = sb("ident", [P, P])
        earlier = sb("earlier", [P, HALF * P])
        zeros = sb("zeros", [P, ROWS * D])
        iota_i = sb("iota_i", [P, cols], I32)
        iota_h = sb("iota_h", [P, cols], F16)
        spare_i = sb("spare_i", [P, HALF], I32)
        spare_f = sb("spare_f", [P, HALF])
        own_i = sb("own_i", [P, 1], I32)
        own_f = sb("own_f", [P, 1])
        w0_sb = sb("w0_sb", [P, D])
        w1_sb = sb("w1_sb", [P, 3, D])
        bias_hi = sb("bias_hi", [3, HALF, D], BF16)
        bias_row = [sb(f"bias_row{n}", [3, HALF, D], BF16) for n in range(2)]
        is_row = sb("is_row", [P, 3])
        ones_row = sb("ones_row", [3, P], BF16)
        gamma_sb = sb("gamma_sb", [P, D])
        beta_sb = sb("beta_sb", [P, D])
        eps_sb = sb("eps_sb", [P, 1])
        row_i = [sb("src_row_i", [P, HALF, P], I32), sb("dst_row_i", [P, HALF, P], I32)]
        row_f = [sb("src_row_f", [P, HALF, P]), sb("dst_row_f", [P, HALF, P])]
        key = [sb("src_key", [P, HALF * P]), sb("dst_key", [P, HALF * P])]
        safe = [sb("src_safe", [P, tiles], I32), sb("dst_safe", [P, tiles], I32)]
        key_i = sb("key_i", [P, tiles], I32)
        place_i = sb("place_i", [P, 3, tiles], I32)
        place = [sb("src_place", [P, 2, tiles]), sb("dst_place", [P, 2, tiles])]
        less_place = sb("less_place", [P, tiles])
        dinv = sb("dinv", [P, cols])
        root = sb("root", [P, cols])
        dense = sb("dense", [P, 3 * SLOTS * ROWS, D])
        xin, ain, dout = ([dense[:, (w * SLOTS + k) * ROWS:(w * SLOTS + k + 1) * ROWS, :] for k in range(SLOTS)]
                          for w in range(3))
        self_in = [sb(f"self_in{h}", [P, HALF, D]) for h in range(2)]
        turned = [sb(f"turned{h}", [P, HALF, P]) for h in range(2)]
        stats = [sb(f"stats{h}", [P, ROWS, 6]) for h in range(2)]
        tmp = [sb(f"tmp{h}", [P, 4, ROWS]) for h in range(2)]
        mean = [sb(f"mean{h}", [P, ROWS]) for h in range(2)]
        spread = [sb(f"spread{h}", [P, ROWS]) for h in range(2)]
        dev = [sb(f"dev{h}", [P, ROWS]) for h in range(2)]
        rstd = [sb(f"rstd{h}", [P, ROWS]) for h in range(2)]
        shift = [sb(f"shift{h}", [P, ROWS]) for h in range(2)]
        hot_p = [sb(f"hot_p{k}", [P, P], F16) for k in range(HOTS)]
        away = [sb(f"away{k}", [P, P], F16) for k in HOTS_ACT]
        hot_c = [sb(f"hot_c{k}", [P, cols], F16) for k in range(HOTS)]
        key_s = [sb(f"key_s{g}", [P, HALF]) for g in range(DEEP)]
        take_a = [sb(f"take_a{g}", [P, HALF], I32) for g in range(DEEP)]
        take_b = [sb(f"take_b{g}", [P, HALF], I32) for g in range(DEEP)]
        give = [sb(f"give{g}", [P, HALF], I32) for g in range(2)]
        same = [[sb(f"same{g}_{j}", [P, (j + 2) * P]) for j in range(HALF)] for g in range(2)]
        before = [sb(f"before{g}", [P, HALF]) for g in range(2)]
        to_spare = [sb(f"to_spare{g}", [P, HALF]) for g in range(2)]
        got_a = [[sb(f"got_a{g}_{k}", [P, D]) for k in range(HALF)] for g in range(DEEP)]
        got_b = [[sb(f"got_b{g}_{k}", [P, D]) for k in range(HALF)] for g in range(DEEP)]
        place_s = [sb(f"place_s{g}", [P, HALF]) for g in range(DEEP)]
        hot_t = [sb(f"hot_t{g}", [P, HALF, P]) for g in range(2)]
        weight = [sb(f"weight{g}", [P, HALF]) for g in range(2)]
        ea = [sb(f"ea{g}", [P, HALF, D]) for g in range(2)]
        in_t = [sb(f"in_t{w}", [P, HALF, P]) for w in range(3)]
        hid = [sb(f"hid{g}", [P, HALF, D]) for g in range(2)]
        hid2 = [sb(f"hid2{g}", [P, HALF, D]) for g in range(2)]
        msg = [sb(f"msg{g}", [P, HALF, D]) for g in range(2)]
        total = [sb(f"total{g}", [P, HALF, D]) for g in range(2)]

        bias = [hid2[n][0:3, :, :] for n in range(2)]
        bias_part = [buffer[0:3, :, :] for buffer in (msg[0], msg[1], ea[1])]
        bias_sum = in_t[0][0:3, :, :]

        junk = [buffer[:, :, :].rearrange("p a b -> p (a b)")[:, 0:cols] for buffer in (*in_t, ea[0])]

        bank = [psum(f"bank{k}") for k in range(8)]
        look = [bank[4 + k][:, :, :].rearrange("p a b -> p (a b)")[:, 0:cols] for k in range(HALF)]
        count_ps = bank[0][:, :, :].rearrange("p a b -> p (a b)")[:, 0:cols]

        s_iota, s_const, s_zero, s_weights = sem("s_iota"), sem("s_const"), sem("s_zero"), sem("s_weights")
        s_rows, s_rowf, s_turn_key = sem("s_rows"), sem("s_rowf"), sem("s_turn_key")
        s_bias = sem("s_bias")
        s_dve, s_place = sem("s_dve"), sem("s_place")
        s_issued = sem("s_issued")
        s_away, s_hot_act = sem("s_away"), sem("s_hot_act")
        s_hot, s_counted, s_root, s_dinv = sem("s_hot"), sem("s_counted"), sem("s_root"), sem("s_dinv")
        s_fill1, s_fill2 = sem("s_fill1"), sem("s_fill2")
        c_early = sem("c_early")
        c_place, c_hot, c_look, c_pick, c_scaled = (
            sem(n) for n in ("c_place", "c_hot", "c_look", "c_pick", "c_scaled"))
        c_stage, c_got, c_turn, c_same, c_step, c_list, c_sum, c_total, c_put = (
            sem("c_stage"), sems("c_got", DEEP * HALF), sem("c_turn"), sem("c_same"), sem("c_step"), sem("c_list"),
            sem("c_sum"), sem("c_total"), sems("c_put", 2))
        d_sums, d_x, d_st = sems("d_sums", SLOTS), sems("d_xin", SLOTS), sems("d_st", SLOTS)
        d_self, d_add, d_scaled, d_turn, d_turned, d_prod, d_pre = (
            sem(n) for n in ("d_self", "d_add", "d_scaled", "d_turn", "d_turned", "d_prod", "d_pre"))
        d_step, d_stat, d_dev, d_rstd, d_shift, d_x1, d_x1_act = (
            sem(n) for n in ("d_step", "d_stat", "d_dev", "d_rstd", "d_shift", "d_x1", "d_x1_act"))
        e_ea, e_got, e_put = sems("e_ea", 2), sems("e_got", DEEP * HALF), sems("e_put", 2)
        e_stage, e_turn, e_same, e_step, e_list, e_sum, e_total = (
            sem(n) for n in ("e_stage", "e_turn", "e_same", "e_step", "e_list", "e_sum", "e_total"))
        e_in, e_ready, e_h, e_stat, e_mom, e_scaled, e_dev, e_rstd, e_norm, e_msg = (
            sem(n) for n in ("e_in", "e_ready", "e_h", "e_stat", "e_mom", "e_scaled", "e_dev", "e_rstd", "e_norm",
                             "e_msg"))
        f_sums, f_x, f_st = sems("f_sums", SLOTS), sems("f_xin", SLOTS), sems("f_st", SLOTS)
        f_add, f_step, f_stat, f_dev, f_rstd, f_shift, f_out, f_out_act = (
            sem(n) for n in ("f_add", "f_step", "f_stat", "f_dev", "f_rstd", "f_shift", "f_out", "f_out_act"))

        def over(eng, count, period, *parts):
            low, high = min(a for a, _ in parts), max(a for a, _ in parts)

            def step(n):
                for a, part in parts:
                    if 0 <= n + a < count:
                        part((n + a) % period, (n + a) // period)

            first = (period - low + period - 1) // period
            tail_from = (count - 1) // period * period
            last = (tail_from - high) // period
            for n in range(-high, first * period):
                step(n)
            with eng.Fori(first, last) as i:
                for q in range(period):
                    for a, part in parts:
                        part((q + a) % period, i + (q + a) // period)
            for n in range(last * period, count - low):
                step(n)

        def since(eng, semaphore, value):
            if not isinstance(value, int) or value > 0:
                eng.wait_ge(semaphore, value)

        def node_rows(table, c):
            if isinstance(c, int) and c == chunks - 1:
                return table[n_nodes - tail_rows:n_nodes, :].rearrange("(p r) d -> p r d", r=ROWS)
            return table[bass.ds(c * chunk, chunk), :].rearrange("(p r) d -> p r d", r=ROWS)

        def held(c):
            return tail_p if isinstance(c, int) and c == chunks - 1 else P

        def uses(k):
            return len(range(k, chunks, SLOTS))

        groups, units = 2 * rounds, 2 * chunks
        early = len(range(DEEP - 1, groups, DEEP))
        last_round = groups // DEEP
        assert (early + groups % DEEP) * HALF <= 3 * SLOTS * ROWS and groups % DEEP < DEEP
        assert tiles % HOTS == 0

        def early_slot(g, r):
            if g == DEEP - 1:
                return r * HALF
            return (early + g) * HALF if isinstance(r, int) and r == last_round else None

        block = ctx.enter_context(nc.Block())

        @block.sync
        def _(sp):
            sp.wait_ge(s_iota, 2)
            for side, ids in enumerate((dst, src)):
                side = 1 - side
                for c in range(HALF):
                    t0, t1 = c * P, min((c + 1) * P, full_tiles)
                    sp.dma_start(row_i[side][0:t1 - t0, c, :],
                                 ids[t0 * P:t1 * P].rearrange("(t e) -> t e", e=P)).then_inc(s_rows, 16)
                at = full_tiles % P
                sp.dma_start(row_i[side][at:at + 1, HALF - 1, 0:tail_edges],
                             ids[full_tiles * P:n_edges].rearrange("(t e) -> t e", t=1)).then_inc(s_rows, 16)
            for to, of in ((w0_sb[:, :], w0), (w1_sb[:, :, :], w1.rearrange("(w p) d -> p w d", p=P)),
                           *((row[:, j, :], b.rearrange("(a d) -> a d", a=1).to_broadcast([3, D]))
                             for row, b in ((bias[0], b0), (bias[1], b1)) for j in range(HALF))):
                sp.dma_start(to, of).then_inc(s_weights, 16)
            for to, of in ((gamma_sb, gamma), (beta_sb, beta)):
                sp.dma_start(to[:, :], of.rearrange("(a d) -> a d", a=1).to_broadcast([P, D])).then_inc(s_weights, 16)

            def zero_chunk(table, i):
                return sp.dma_start(table[bass.ds(i * chunk, chunk), :].rearrange("(p r) d -> p r d", r=ROWS),
                                    zeros[:, :].rearrange("p (r d) -> p r d", d=D))

            def zero_spare(table):
                return sp.dma_start(table[chunks * chunk:table_rows, :],
                                    zeros[:, 0:(table_rows - chunks * chunk) // P * D])

            sp.wait_ge(s_zero, 1)
            with sp.Fori(0, chunks) as i:
                zero_chunk(agg, i).then_inc(s_fill1, 16)
            zero_spare(agg).then_inc(s_fill1, 16)

            zero_spare(osum).then_inc(s_fill2, 16)
            with sp.Fori(1, chunks + 1) as i:
                sp.wait_ge(c_sum, i * 2 - 1)
                zero_chunk(osum, i - 1).then_inc(s_fill2, 16)

            for s in c_put:
                sp.wait_ge(s, 16 * HALF * rounds)

            def load_d(k, i):
                c = i * SLOTS + k
                since(sp, d_turn, 2 * (c - SLOTS) + 2)
                sp.dma_start(ain[k][0:held(c), :, :], node_rows(agg, c)).then_inc(d_sums[k], 16)
                since(sp, d_x1, c - SLOTS + 1)
                since(sp, d_x1_act, c - SLOTS + 1)
                sp.dma_start(xin[k][0:held(c), :, :], node_rows(x, c)).then_inc(d_x[k], 16)

            over(sp, chunks, SLOTS, (0, load_d))

            def load_e(g, r):
                n = r * 2 + g
                since(sp, e_in, n - 1)
                if isinstance(n, int) and n >= groups - 2:
                    here = min(HALF, full_tiles - n * HALF)
                    if here > 0:
                        sp.dma_start(ea[g][:, 0:here, :], edge_attr[n * HALF * P:(n * HALF + here) * P, :].rearrange(
                            "(k p) d -> p k d", p=P)).then_inc(e_ea[g], 16)
                    if 0 <= here < HALF and tail_edges:
                        sp.dma_start(ea[g][0:tail_edges, here, :],
                                     edge_attr[full_tiles * P:n_edges, :]).then_inc(e_ea[g], 16)
                else:
                    sp.dma_start(ea[g][:, :, :], edge_attr[bass.ds(n * HALF * P, HALF * P), :].rearrange(
                        "(k p) d -> p k d", p=P)).then_inc(e_ea[g], 16)

            over(sp, groups, 2, (0, load_e))

            for k in range(SLOTS):
                sp.wait_ge(d_st[k], 16 * uses(k))
            for k in range(SLOTS):
                sp.dma_start(xin[k][:, :, :], node_rows(x1_dram, k)).then_inc(f_x[k], 16)
            for s in e_put:
                sp.wait_ge(s, 16 * HALF * rounds)

            def load_f(k, i):
                c = i * SLOTS + k
                since(sp, f_add, c - SLOTS + 1)
                sp.dma_start(ain[k][0:held(c), :, :], node_rows(osum, c)).then_inc(f_sums[k], 16)
                if not isinstance(c, int) or c >= SLOTS:
                    sp.wait_ge(f_out, c - SLOTS + 1)
                    sp.wait_ge(f_out_act, c - SLOTS + 1)
                    sp.dma_start(xin[k][0:held(c), :, :], node_rows(x1_dram, c)).then_inc(f_x[k], 16)

            over(sp, chunks, SLOTS, (0, load_f))

            for k in range(SLOTS):
                sp.wait_ge(f_st[k], 16 * uses(k))

        @block.gpsimd
        def _(pool):
            for side in range(2):
                nc.gpsimd.iota(row_i[side][:, HALF - 1, :], pattern=[[1, P]], base=spare,
                               channel_multiplier=0).then_inc(s_iota, 1)
            nc.gpsimd.iota(iota_i[:, :], pattern=[[1, cols]], base=0, channel_multiplier=0).then_inc(s_iota, 1)
            nc.gpsimd.iota(spare_i[:, :], pattern=[[P, HALF]], base=spare + P, channel_multiplier=1).then_inc(s_iota, 1)
            nc.gpsimd.iota(own_i[:, :], pattern=[[1, 1]], base=0, channel_multiplier=1).then_inc(s_iota, 1)
            nc.gpsimd.memset(ident[:, :], 0.0).then_inc(s_const, 1)
            nc.gpsimd.memset(earlier[:, :], 1.0).then_inc(s_const, 1)
            nc.gpsimd.memset(eps_sb[:, :], EPS).then_inc(s_const, 1)
            nc.gpsimd.memset(ones_row[:, :], 1.0).then_inc(s_const, 1)
            pool.wait_ge(s_const, 4)
            nc.gpsimd.affine_select(out=ident[:, :], in_=ident[:, :], compare_op=ALU.not_equal, fill=1.0, base=0,
                                    pattern=[[-1, P]], channel_multiplier=1).then_inc(s_const, 1)
            nc.gpsimd.affine_select(out=earlier[:, (HALF - 1) * P:HALF * P],
                                    in_=earlier[:, (HALF - 1) * P:HALF * P], compare_op=ALU.is_gt, fill=0.0, base=0,
                                    pattern=[[-1, P]], channel_multiplier=1).then_inc(s_const, 1)
            nc.gpsimd.memset(zeros[:, :], 0.0).then_inc(s_zero, 1)

            def take(table, lists, staged, into, got, used, k):
                def part(g, r):
                    n = r * DEEP + g
                    if staged is not None and k == 0:
                        since(pool, used, n - DEEP + 1)
                        pool.wait_ge(staged, n + 1)
                        pool.sem_inc(s_issued, 1)
                    nc.gpsimd.indirect_dma_start(
                        into[g][k][:, :], None, table, bass.IndirectOffsetOnAxis(lists[g][:, k:k + 1], 0),
                        bounds_check=n_nodes - 1, oob_is_err=True).then_inc(got[g * HALF + k], 16)
                return part

            def put(table, listed, copied, added, k):
                def part(g, r):
                    n, r, g = r * DEEP + g, r * (DEEP // 2) + g // 2, g % 2
                    if k == 0:
                        pool.wait_ge(listed, n + 1)
                        pool.wait_ge(copied, n + 1)
                        since(pool, added[1 - g], (r + g) * HALF * 16)
                        pool.sem_inc(s_issued, 1)
                    nc.gpsimd.indirect_dma_start(
                        table, bass.IndirectOffsetOnAxis(give[g][:, k:k + 1], 0), total[g][:, k, :], None,
                        bounds_check=table_rows - 1, oob_is_err=True, compute_op=ALU.add).then_inc(added[g], 16)
                return part

            def first_put(g, r):
                if isinstance(r, int) and r == 0 and g == 0:
                    pool.wait_ge(s_fill1, 16 * (chunks + 1))
                put(agg, c_list, c_total, c_put, 0)(g, r)

            def take_c(k):
                def part(g, r):
                    if early_slot(g, r) is None:
                        take(x, take_a, c_stage, got_a, c_got, c_scaled, k)(g, r)
                return part

            for g in range(DEEP - 1):
                for k in range(HALF):
                    take_c(k)(g, 0)
            for n in (*range(DEEP - 1, groups, DEEP), *range(last_round * DEEP, groups)):
                for k in range(HALF):
                    t = n * HALF + k
                    nc.gpsimd.indirect_dma_start(
                        dense[:, early_slot(n % DEEP, n // DEEP) + k, :], None, x,
                        bass.IndirectOffsetOnAxis(safe[0][:, t:t + 1], 0),
                        bounds_check=n_nodes - 1, oob_is_err=True).then_inc(c_early, 16)

            def take_rest(k, late):
                def part(g, r):
                    if (not isinstance(r, int) or r > 0) and late == (k + g >= DEEP - 1):
                        take_c(k)(g, r)
                return part

            over(pool, groups, DEEP, (0, first_put),
                 *((0, put(agg, c_list, c_total, c_put, k)) for k in range(1, HALF)),
                 *((2, take_rest(k, True)) for k in range(HALF)), *((3, take_rest(k, False)) for k in range(HALF)))

            def add_d(q, i):
                k, h, u = q // 2, q % 2, i * 2 * SLOTS + q
                part = slice(h * HALF, (h + 1) * HALF)
                if h == 0:
                    pool.wait_ge(d_x[k], i * 16 + 16)
                since(pool, d_add, u - 1)
                nc.gpsimd.tensor_tensor(self_in[h][:, :, :], xin[k][:, part, :],
                                        dinv[:, bass.ds(u * HALF, HALF)].unsqueeze(2).to_broadcast([P, HALF, D]),
                                        ALU.mult).then_inc(d_self, 1)
                if h == 0:
                    pool.wait_ge(d_sums[k], i * 16 + 16)
                pool.wait_ge(d_self, u + 1)
                nc.gpsimd.tensor_tensor(ain[k][:, part, :], ain[k][:, part, :], self_in[h][:, :, :],
                                        ALU.add).then_inc(d_add, 1)

            over(pool, units, 2 * SLOTS, (0, add_d))

            for k in range(SLOTS):
                pool.wait_ge(d_st[k], 16 * uses(k))
            pool.wait_ge(s_fill2, 16 * (chunks + 1))
            parts = []
            for k in range(HALF):
                parts.append((-1, put(osum, e_list, e_total, e_put, k)))
            for k in range(HALF):
                parts.append((3, take(x1_dram, take_a, e_stage, got_a, e_got, e_in, k)))
                parts.append((3, take(x1_dram, take_b, None, got_b, e_got, e_in, k)))
            over(pool, groups, DEEP, *parts)

            def add_f(k, i):
                pool.wait_ge(f_sums[k], i * 16 + 16)
                pool.wait_ge(f_x[k], i * 16 + 16)
                nc.gpsimd.tensor_tensor(xin[k][:, :, :], ain[k][:, :, :], xin[k][:, :, :], ALU.add).then_inc(f_add, 1)

            over(pool, chunks, SLOTS, (0, add_f))

        @block.tensor
        def _(pe):
            pe.wait_ge(s_const, 6)
            pe.wait_ge(s_rowf, 2)
            for side in range(2):
                for c in range(HALF):
                    n = min(P, tiles - c * P)
                    last = nc.tensor.transpose(bank[1 + side][:, c, 0:n], row_f[side][0:n, c, :], ident[0:n, 0:n])
                last.then_inc(s_turn_key, 1)

            def count(k, i):
                t = i * HOTS + k
                pe.wait_ge(s_hot, t + 1)
                if k in HOTS_ACT:
                    pe.wait_ge(s_hot_act, i * len(HOTS_ACT) + HOTS_ACT.index(k) + 1)
                nc.tensor.matmul(count_ps, hot_p[k][:, :], hot_c[k][:, :], start=isinstance(t, int) and t == 0,
                                 stop=isinstance(t, int) and t == tiles - 1).then_inc(s_counted, 1)

            over(pe, tiles, HOTS, (0, count))

            def turn_keys(staged, compared, turn):
                def part(g, r):
                    n = r * DEEP + g
                    pe.wait_ge(staged, n + 1)
                    since(pe, compared, n - 1)
                    for k in range(HALF):
                        last = nc.tensor.transpose(bank[g % 2][:, k, :], key_s[g][:, k:k + 1].to_broadcast([P, P]),
                                                   ident[:, :])
                    last.then_inc(turn, 1)
                return part

            def sum_group(of, g, h, place_of):
                for t in range(HALF):
                    for j in range(t, HALF):
                        at = (j + 1) * P if j == t else t * P
                        last = nc.tensor.matmul(place_of[:, t, :], same[h][j][:, at:at + P], of[h][:, j, :],
                                                start=j == t, stop=j == HALF - 1)
                return last

            pe.wait_ge(s_root, 1)
            pe.wait_ge(s_dinv, 1)

            def turn_place(g, r):
                n = r * DEEP + g
                pe.wait_ge(c_stage, n + 1)
                since(pe, c_hot, n)
                for k in range(HALF):
                    last = nc.tensor.transpose(bank[2][:, k, :], place_s[g][:, k:k + 1].to_broadcast([P, P]),
                                               ident[:, :])
                last.then_inc(c_place, 1)

            def look_up(g, r):
                n = r * DEEP + g
                pe.wait_ge(c_hot, n + 1)
                since(pe, c_pick, n)
                for k in range(HALF):
                    last = nc.tensor.matmul(look[k], hot_t[g % 2][:, k, :], dinv[:, :], start=True, stop=True)
                last.then_inc(c_look, 1)

            def sum_c(g, r):
                n = r * DEEP + g
                pe.wait_ge(c_same, n + 1)
                pe.wait_ge(c_scaled, n + 1)
                since(pe, c_total, n)
                sum_group(hid, g, g % 2, bank[3]).then_inc(c_sum, 1)

            over(pe, groups, DEEP, (2, look_up), (0, sum_c), (3, turn_place), (3, turn_keys(c_stage, c_same, c_turn)))

            pe.wait_ge(s_weights, (4 + 2 * HALF) * 16)
            pe.wait_ge(s_bias, 2)
            pe.wait_ge(c_same, groups)
            pe.wait_ge(c_total, groups)

            def turn_d(q, i):
                k, h, u = q // 2, q % 2, i * 2 * SLOTS + q
                pe.wait_ge(d_scaled, u + 1)
                since(pe, d_turned, u - 1)
                for j in range(HALF):
                    last = nc.tensor.transpose(bank[h][:, j, :], ain[k][:, h * HALF + j, :], ident[:, :])
                last.then_inc(d_turn, 1)

            def prod_d(q, i):
                h, u = q % 2, i * 2 * SLOTS + q
                pe.wait_ge(d_turned, u + 1)
                since(pe, d_pre, u - 1)
                for j in range(HALF):
                    nc.tensor.matmul(bank[2 + h][:, j, :], turned[h][:, j, :], w0_sb[:, :], start=j == 0, stop=False,
                                     skip_group_check=True)
                nc.tensor.matmul(bank[2 + h][:, :, :], ones_row[:, :], bias_row[0][:, :, :], start=False, stop=True,
                                 skip_group_check=True).then_inc(d_prod, 1)

            over(pe, units, 2 * SLOTS, (2, turn_d), (1, prod_d))

            pe.wait_ge(d_pre, units)

            def turn_in(g, r):
                n, v, h = r * DEEP + g, r * (DEEP // 2) + g // 2, g % 2
                since(pe, e_ready, n)
                for w, rows in enumerate((got_a, got_b)):
                    for k in range(HALF):
                        pe.wait_ge(e_got[g * HALF + k], r * 32 + 32)
                        nc.tensor.transpose(bank[4 + w][:, k, :], rows[g][k][:, :], ident[:, :])
                loads = 1
                if isinstance(n, int) and n >= groups - 2:
                    here = full_tiles - n * HALF
                    loads = (1 if here > 0 else 0) + (1 if 0 <= here < HALF and tail_edges else 0)
                pe.wait_ge(e_ea[h], v * 16 + loads * 16)
                for k in range(HALF):
                    last = nc.tensor.transpose(bank[6][:, k, :], ea[h][:, k, :], ident[:, :])
                last.then_inc(e_in, 1)

            def hidden(g, r):
                n = r * DEEP + g
                pe.wait_ge(e_ready, n + 1)
                since(pe, e_scaled, n)
                for k in range(HALF):
                    for w in range(3):
                        nc.tensor.matmul(bank[7][:, k, :], in_t[w][:, k, :], w1_sb[:, w, :],
                                         start=k == 0 and w == 0, stop=False, skip_group_check=True)
                last = nc.tensor.matmul(bank[7][:, :, :], ones_row[:, :], bias_row[1][:, :, :], start=False, stop=True,
                                        skip_group_check=True)
                last.then_inc(e_h, 1)

            def sum_e(g, r):
                n, g = r * DEEP + g, g % 2
                pe.wait_ge(e_msg, n + 1)
                since(pe, e_total, n - 1)
                sum_group(msg, g, g, bank[2 + g]).then_inc(e_sum, 1)

            over(pe, groups, DEEP, (1, hidden), (0, sum_e), (2, turn_keys(e_stage, e_same, e_turn)), (2, turn_in))

        @block.scalar
        def _(act):
            act.wait_ge(s_place, 1)

            def distance(k, i):
                t = i * HOTS + HOTS_ACT[k]
                since(act, s_hot_act, (i - 1) * len(HOTS_ACT) + k + 1)
                nc.scalar.activation(away[k][:, :], iota_h[:, 0:P], ACT.Abs,
                                     bias=less_place[:, bass.ds(t, 1)]).then_inc(s_away, 1)

            def hot_act(k, i):
                t = i * HOTS + HOTS_ACT[k]
                act.wait_ge(s_away, i * len(HOTS_ACT) + k + 1)
                since(act, s_counted, t - HOTS + 1)
                nc.scalar.activation(hot_p[HOTS_ACT[k]][:, :], away[k][:, :], ACT.Relu, bias=1.0,
                                     scale=-1.0).then_inc(s_hot_act, 1)

            over(act, tiles // HOTS * len(HOTS_ACT), len(HOTS_ACT), (1, distance), (0, hot_act))

            act.wait_ge(s_counted, tiles)
            nc.scalar.activation(root[:, :], count_ps, ACT.Sqrt, bias=1.0).then_inc(s_root, 1)

            def copy_sums(summed, added, copied, banks):
                def part(g, r):
                    g, r = g % 2, r * (DEEP // 2) + g // 2
                    act.wait_ge(summed, r * 2 + g + 1)
                    since(act, added[g], r * HALF * 16)
                    nc.scalar.copy(total[g][:, :, :], banks[g][:, :, :]).then_inc(copied, 1)
                return part

            def scale_c(g, r):
                n, h = r * DEEP + g, g % 2
                act.wait_ge(c_pick, n + 1)
                since(act, c_sum, n - 1)
                at = early_slot(g, r)
                for k in range(HALF):
                    if at is None:
                        act.wait_ge(c_got[g * HALF + k], r * 16 + 16)
                        rows = got_a[g][k][:, :]
                    else:
                        rows = dense[:, bass.ds(at + k, 1), :].rearrange("p a b -> p (a b)")
                    last = nc.scalar.activation(hid[h][:, k, :], rows, ACT.Copy,
                                                scale=weight[h][:, k:k + 1])
                last.then_inc(c_scaled, 1)

            act.wait_ge(c_early, 16 * (early + groups % DEEP) * HALF)
            over(act, groups, DEEP, (0, copy_sums(c_sum, c_put, c_total, (bank[3], bank[3]))), (1, scale_c))

            def scale_d(q, i):
                k, h, u = q // 2, q % 2, i * 2 * SLOTS + q
                act.wait_ge(d_add, u + 1)
                for j in range(HALF):
                    rows = ain[k][:, h * HALF + j, :]
                    last = nc.scalar.activation(rows, rows, ACT.Copy, scale=dinv[:, bass.ds(u * HALF + j, 1)])
                last.then_inc(d_scaled, 1)

            def turned_d(q, i):
                h, u = q % 2, i * 2 * SLOTS + q
                act.wait_ge(d_turn, u + 1)
                since(act, d_prod, u - 1)
                nc.scalar.copy(turned[h][:, :, :], bank[h][:, :, :]).then_inc(d_turned, 1)

            def dev_d(q, i):
                c, k = i * SLOTS + q // 2, q // 2 % 2
                if q % 2 == 1:
                    act.wait_ge(d_stat, c + 1)
                    since(act, d_rstd, c - 1)
                    nc.scalar.activation(dev[k][:, :], spread[k][:, :], ACT.Sqrt, bias=eps_sb[:, :],
                                         scale=1.0 / D).then_inc(d_dev, 1)

            def normal_act(half):
                def part(q, i):
                    k, c = q // 2, i * SLOTS + q // 2
                    if q % 2 == 0:
                        return
                    if half == 0:
                        act.wait_ge(d_shift, c + 1)
                        since(act, d_st[k], i * 16)
                    for j in ACT_BLOCKS[half]:
                        last = nc.scalar.activation(dout[k][:, j, :], xin[k][:, j, :], ACT.Identity,
                                                    bias=shift[k % 2][:, j:j + 1], scale=rstd[k % 2][:, j:j + 1])
                    if half == 1:
                        last.then_inc(d_x1_act, 1)
                return part

            def store_d(q, i):
                k, c = q // 2, i * SLOTS + q // 2
                if q % 2 == 1:
                    act.wait_ge(d_x1_act, c + 1)
                    act.wait_ge(d_x1, c + 1)
                    act.dma_start(node_rows(x1_dram, c), dout[k][0:held(c), :, :]).then_inc(d_st[k], 16)

            over(act, units, 2 * SLOTS, (3, scale_d), (2, turned_d), (-1, normal_act(0)), (-2, normal_act(1)),
                 (0, dev_d), (-3, store_d))

            def ready(g, r):
                n = r * DEEP + g
                act.wait_ge(e_in, n + 1)
                since(act, e_h, n)
                for w in range(3):
                    last = nc.scalar.copy(in_t[w][:, :, :], bank[4 + w][:, :, :])
                last.then_inc(e_ready, 1)

            def dev_e(g, r):
                n, g = r * DEEP + g, g % 2
                act.wait_ge(e_stat, n + 1)
                since(act, e_rstd, n - 1)
                nc.scalar.activation(dev[g][:, 0:HALF], spread[g][:, 0:HALF], ACT.Sqrt, bias=eps_sb[:, :],
                                     scale=1.0 / D).then_inc(e_dev, 1)

            def messages(g, r):
                n, g = r * DEEP + g, g % 2
                act.wait_ge(e_norm, n + 1)
                since(act, e_sum, n - 1)
                nc.scalar.activation(msg[g][:, :, :], hid2[g][:, :, :], ACT.Relu).then_inc(e_msg, 1)

            over(act, groups, DEEP, (0, dev_e), (0, messages),
                 (0, copy_sums(e_sum, e_put, e_total, (bank[2], bank[3]))), (2, ready))

            def dev_f(k, i):
                c = i * SLOTS + k
                act.wait_ge(f_stat, c + 1)
                since(act, f_rstd, c - 1)
                nc.scalar.activation(dev[k % 2][:, :], spread[k % 2][:, :], ACT.Sqrt, bias=eps_sb[:, :],
                                     scale=1.0 / D).then_inc(f_dev, 1)

            def normal_f_act(k, i):
                act.wait_ge(f_shift, i * SLOTS + k + 1)
                since(act, f_st[k], i * 16)
                for j in range(ACT_LAST):
                    last = nc.scalar.activation(dout[k][:, j, :], xin[k][:, j, :], ACT.Identity,
                                                bias=shift[k % 2][:, j:j + 1], scale=rstd[k % 2][:, j:j + 1])
                last.then_inc(f_out_act, 1)

            def store_f(k, i):
                c = i * SLOTS + k
                act.wait_ge(f_out_act, c + 1)
                act.wait_ge(f_out, c + 1)
                act.dma_start(node_rows(out, c), dout[k][0:held(c), :, :]).then_inc(f_st[k], 16)

            over(act, chunks, SLOTS, (0, normal_f_act), (1, dev_f), (0, store_f))

        @block.vector
        def _(dve):
            made = [0]

            def link(ins):
                made[0] += 1
                ins.then_inc(s_dve, 1)
                dve.wait_ge(s_dve, made[0])

            dve.wait_ge(s_iota, 5)
            nc.vector.tensor_copy(iota_h[:, :], iota_i[:, :])
            nc.vector.tensor_copy(own_f[:, :], own_i[:, :])
            link(nc.vector.tensor_copy(spare_f[:, :], spare_i[:, :]))
            dve.wait_ge(s_rows, 16 * 2 * (HALF + 1))
            for side in range(2):
                nc.vector.tensor_copy(row_f[side][:, 0:HALF - 1, :], row_i[side][:, 0:HALF - 1, :])
                n = tiles - (HALF - 1) * P
                nc.vector.tensor_copy(row_f[side][0:n, HALF - 1, :],
                                      row_i[side][0:n, HALF - 1, :]).then_inc(s_rowf, 1)
            for side in range(2):
                dve.wait_ge(s_turn_key, side + 1)
                link(nc.vector.tensor_copy(key[side][:, 0:tiles],
                                           bank[1 + side][:, :, :].rearrange("p a b -> p (a b)")[:, 0:tiles]))
                link(nc.vector.tensor_scalar(safe[side][:, :], key[side][:, 0:tiles], float(n_nodes - 1), None,
                                             ALU.min))
            for side in range(2):
                link(nc.vector.tensor_copy(key_i[:, :], key[side][:, 0:tiles]))
                nc.vector.tensor_scalar(place_i[:, 0, :], key_i[:, :], LOG_ROWS, P - 1, ALU.arith_shift_right,
                                        ALU.bitwise_and)
                nc.vector.tensor_scalar(place_i[:, 1, :], key_i[:, :], LOG_CHUNK, None, ALU.arith_shift_right)
                link(nc.vector.tensor_scalar(place_i[:, 2, :], key_i[:, :], ROWS - 1, None, ALU.bitwise_and))
                nc.vector.tensor_copy(place[side][:, 0, :], place_i[:, 0, :])
                link(nc.vector.scalar_tensor_tensor(out=place[side][:, 1, :], in0=place_i[:, 1, :],
                                                    scalar=float(ROWS), in1=place_i[:, 2, :], op0=ALU.mult,
                                                    op1=ALU.add))

            def stage(key_side, lists, got, uses, compared, staged, listed=DEEP):
                def part(g, r):
                    n = r * DEEP + g
                    since(dve, compared, n - DEEP + 1)
                    for side, to in lists if g < listed else ():
                        for k in range(HALF):
                            since(dve, got[g * HALF + k], r * uses * 16)
                        nc.vector.tensor_copy(to[g][:, :], safe[side][:, bass.ds(n * HALF, HALF)])
                    if key_side == 1:
                        nc.vector.tensor_copy(place_s[g][:, :], place[0][:, 0, bass.ds(n * HALF, HALF)])
                    nc.vector.tensor_copy(key_s[g][:, :], key[key_side][:, bass.ds(n * HALF, HALF)]).then_inc(
                        staged, 1)
                return part

            nc.vector.tensor_scalar(less_place[:, :], place[1][:, 0, :], -1.0, None, ALU.mult).then_inc(s_place, 1)

            stage_c = stage(1, ((0, take_a),), c_got, 1, c_same, c_stage, DEEP - 1)
            for g in range(DEEP):
                stage_c(g, 0)

            def one_hot(k, i):
                t, k = i * 2 * HOTS + k, k % HOTS
                if k % 4 == 0:
                    since(dve, s_counted, t - HOTS + 4)
                if k not in HOTS_ACT:
                    nc.vector.tensor_scalar(hot_p[k][:, :], iota_h[:, 0:P], place[1][:, 0, bass.ds(t, 1)], None,
                                            ALU.is_equal)
                nc.vector.tensor_scalar(hot_c[k][:, :], iota_h[:, :], place[1][:, 1, bass.ds(t, 1)], None,
                                        ALU.is_equal).then_inc(s_hot, 1)

            over(dve, tiles, 2 * HOTS, (0, one_hot))

            dve.wait_ge(s_root, 1)
            nc.vector.reciprocal(dinv[:, :], root[:, :]).then_inc(s_dinv, 1)
            dve.wait_ge(s_dinv, 1)

            def compare(turn, summed, compared):
                def part(g, r):
                    n, h = r * DEEP + g, g % 2
                    dve.wait_ge(turn, n + 1)
                    since(dve, summed, n - 1)
                    row = bank[h][:, :, :].rearrange("p a b -> p (a b)")
                    for j in range(HALF):
                        nc.vector.scalar_tensor_tensor(
                            out=same[h][j][:, 0:(j + 1) * P], in0=row[:, 0:(j + 1) * P], scalar=key_s[g][:, j:j + 1],
                            in1=earlier[:, (HALF - 1 - j) * P:HALF * P], op0=ALU.is_equal, op1=ALU.mult,
                            accum_out=before[h][:, j:j + 1])
                        last = nc.vector.tensor_scalar(same[h][j][:, (j + 1) * P:(j + 2) * P],
                                                       row[:, j * P:(j + 1) * P], key_s[g][:, j:j + 1], None,
                                                       ALU.is_equal)
                    last.then_inc(compared, 1)
                return part

            def rows_to_add(key_side, compared, stepped, added, listed):
                def part(g, r):
                    n, r, g = r * DEEP + g, r * (DEEP // 2) + g // 2, g % 2
                    keys = key[key_side][:, bass.ds(n * HALF, HALF)]
                    dve.wait_ge(compared, n + 1)
                    nc.vector.tensor_scalar(before[g][:, :], before[g][:, :], 1.0, None, ALU.min)
                    nc.vector.tensor_tensor(to_spare[g][:, :], spare_f[:, :], keys,
                                            ALU.subtract).then_inc(stepped, 1)
                    dve.wait_ge(stepped, n * 2 + 1)
                    nc.vector.tensor_tensor(to_spare[g][:, :], to_spare[g][:, :], before[g][:, :],
                                            ALU.mult).then_inc(stepped, 1)
                    dve.wait_ge(stepped, n * 2 + 2)
                    since(dve, added[g], r * HALF * 16)
                    nc.vector.tensor_tensor(give[g][:, :], to_spare[g][:, :], keys,
                                            ALU.add).then_inc(listed, 1)
                return part

            def moments(h, n, step, done, at, finished):
                m0, v0, m1, v1 = (stats[h][:, 0:n, c] for c in (1, 2, 4, 5))
                dve.wait_ge(done, at + step + 1)
                if step == 0:
                    nc.vector.tensor_tensor(tmp[h][:, 0, 0:n], m0, m1, ALU.add)
                    nc.vector.tensor_tensor(tmp[h][:, 1, 0:n], m0, m1, ALU.subtract)
                    nc.vector.tensor_tensor(tmp[h][:, 2, 0:n], v0, v1, ALU.add).then_inc(done, 1)
                elif step == 1:
                    nc.vector.tensor_scalar(mean[h][:, 0:n], tmp[h][:, 0, 0:n], 0.5, None, ALU.mult)
                    nc.vector.tensor_tensor(tmp[h][:, 3, 0:n], tmp[h][:, 1, 0:n], tmp[h][:, 1, 0:n],
                                            ALU.mult).then_inc(done, 1)
                else:
                    nc.vector.scalar_tensor_tensor(out=spread[h][:, 0:n], in0=tmp[h][:, 3, 0:n], scalar=D / 4.0,
                                                   in1=tmp[h][:, 2, 0:n], op0=ALU.mult,
                                                   op1=ALU.add).then_inc(finished, 1)

            def hot_places(g, r):
                n, h = r * DEEP + g, g % 2
                dve.wait_ge(c_place, n + 1)
                since(dve, c_look, n - 1)
                nc.vector.tensor_scalar(hot_t[h][:, :, :], bank[2][:, :, :], own_f[:, 0:1], None,
                                        ALU.is_equal).then_inc(c_hot, 1)

            def pick(g, r):
                n, h = r * DEEP + g, g % 2
                dve.wait_ge(c_look, n + 1)
                since(dve, c_scaled, n - 1)
                for k in range(HALF):
                    last = nc.vector.scalar_tensor_tensor(
                        out=junk[k], in0=iota_h[:, :], scalar=place[0][:, 1, bass.ds(n * HALF + k, 1)],
                        in1=look[k], op0=ALU.is_equal, op1=ALU.mult, accum_out=weight[h][:, k:k + 1])
                last.then_inc(c_pick, 1)

            def stage_rest(g, r):
                if not isinstance(r, int) or r > 0:
                    stage_c(g, r)

            over(dve, groups, DEEP, (1, pick), (2, hot_places), (1, compare(c_turn, c_sum, c_same)),
                 (0, rows_to_add(1, c_same, c_step, c_put, c_list)), (4, stage_rest))

            dve.wait_ge(s_weights, (4 + 2 * HALF) * 16)
            for m in range(3):
                last = nc.vector.tensor_scalar(is_row[:, m:m + 1], own_f[:, :], float(m), None, ALU.is_equal)
            link(last)
            for b in range(2):
                rest = bias[b]
                for m in range(2):
                    link(nc.vector.tensor_copy(bias_hi[:, :, :], rest))
                    link(nc.vector.tensor_copy(bias_part[m], bias_hi[:, :, :]))
                    to = bias_part[2] if m == 1 else bias_sum
                    link(nc.vector.tensor_tensor(to, rest, bias_part[m], ALU.subtract))
                    rest = to
                link(nc.vector.tensor_scalar(bias_sum, bias_part[0], is_row[0:3, 0:1], None, ALU.mult))
                for m in (1, 2):
                    link(nc.vector.scalar_tensor_tensor(
                        out=bias_sum, in0=bias_part[m], scalar=is_row[0:3, m:m + 1], in1=bias_sum,
                        op0=ALU.mult, op1=ALU.add))
                nc.vector.tensor_copy(bias_row[b][:, :, :], bias_sum).then_inc(s_bias, 1)
                dve.wait_ge(s_bias, b + 1)

            def residual(q, i):
                k, h, u = q // 2, q % 2, i * 2 * SLOTS + q
                part = slice(h * HALF, (h + 1) * HALF)
                since(dve, d_self, u + 1)
                dve.wait_ge(d_prod, u + 1)
                nc.vector.scalar_tensor_tensor(
                    out=xin[k][:, part, :], in0=bank[2 + h][:, :, :], scalar=0.0, in1=xin[k][:, part, :], op0=ALU.max,
                    op1=ALU.add).then_inc(d_pre, 1)

            def stats_d(q, i):
                k, h, u = q // 2, q % 2, i * 2 * SLOTS + q
                dve.wait_ge(d_pre, u + 1)
                for j in range(h * HALF, (h + 1) * HALF):
                    last = nc.vector.bn_stats(stats[k % 2][:, j, :], xin[k][:, j, :])
                if h == 1:
                    last.then_inc(d_step, 1)

            def moments_d(step):
                def part(q, i):
                    if q % 2 == 1:
                        moments(q // 2 % 2, ROWS, step, d_step, (i * SLOTS + q // 2) * 3, d_stat)
                return part

            def rstd_d(q, i):
                k, c = q // 2 % 2, i * SLOTS + q // 2
                if q % 2 == 1:
                    dve.wait_ge(d_dev, c + 1)
                    since(dve, d_x1_act, c - 1)
                    nc.vector.reciprocal(rstd[k][:, :], dev[k][:, :]).then_inc(d_rstd, 1)

            def shift_d(q, i):
                k, c = q // 2 % 2, i * SLOTS + q // 2
                if q % 2 == 1:
                    dve.wait_ge(d_rstd, c + 1)
                    nc.vector.scalar_tensor_tensor(out=shift[k][:, :], in0=mean[k][:, :], scalar=-1.0,
                                                   in1=rstd[k][:, :], op0=ALU.mult, op1=ALU.mult).then_inc(d_shift, 1)

            def normal_d(j):
                def part(q, i):
                    k = q // 2
                    if q % 2 == 0:
                        return
                    if j == DVE_BLOCKS[0][0]:
                        since(dve, d_st[k], i * 16)
                    done = nc.vector.tensor_scalar(dout[k][:, j, :], xin[k][:, j, :], mean[k % 2][:, j:j + 1],
                                                   rstd[k % 2][:, j:j + 1], ALU.subtract, ALU.mult)
                    if j == ROWS - 1:
                        done.then_inc(d_x1, 1)
                return part

            over(dve, units, 2 * SLOTS, (0, residual), (-1, rstd_d), (0, stats_d), (-1, shift_d), (-2, normal_d(5)),
                 (0, moments_d(0)), (-1, normal_d(2)), (-2, normal_d(6)), (0, moments_d(1)), (-1, normal_d(3)),
                 (-2, normal_d(7)), (0, moments_d(2)))

            def normal_e(g, r):
                n, g = r * DEEP + g, g % 2
                dve.wait_ge(e_h, n + 1)
                for k in range(HALF):
                    last = nc.vector.bn_stats(stats[g][:, k, :], bank[7][:, k, :])
                last.then_inc(e_mom, 1)
                for step in range(3):
                    moments(g, HALF, step, e_mom, n * 3, e_stat)
                dve.wait_ge(e_stat, n + 1)
                for k in range(HALF):
                    last = nc.vector.scalar_tensor_tensor(
                        out=hid[g][:, k, :], in0=bank[7][:, k, :], scalar=mean[g][:, k:k + 1], in1=gamma_sb[:, :],
                        op0=ALU.subtract, op1=ALU.mult)
                last.then_inc(e_scaled, 1)
                dve.wait_ge(e_dev, n + 1)
                nc.vector.reciprocal(rstd[g][:, 0:HALF], dev[g][:, 0:HALF]).then_inc(e_rstd, 1)
                dve.wait_ge(e_rstd, n + 1)
                dve.wait_ge(e_scaled, n + 1)
                since(dve, e_msg, n - 1)
                for k in range(HALF):
                    last = nc.vector.scalar_tensor_tensor(
                        out=hid2[g][:, k, :], in0=hid[g][:, k, :], scalar=rstd[g][:, k:k + 1], in1=beta_sb[:, :],
                        op0=ALU.mult, op1=ALU.add)
                last.then_inc(e_norm, 1)

            over(dve, groups, DEEP, (0, normal_e), (0, rows_to_add(0, e_same, e_step, e_put, e_list)),
                 (1, compare(e_turn, e_sum, e_same)),
                 (4, stage(0, ((0, take_a), (1, take_b)), e_got, 2, e_same, e_stage)))

            def stats_f(k, i):
                c = i * SLOTS + k
                dve.wait_ge(f_add, c + 1)
                for j in range(ROWS):
                    last = nc.vector.bn_stats(stats[k % 2][:, j, :], xin[k][:, j, :])
                last.then_inc(f_step, 1)

            def moments_f(step):
                def part(k, i):
                    moments(k % 2, ROWS, step, f_step, (i * SLOTS + k) * 3, f_stat)
                return part

            def rstd_f(k, i):
                dve.wait_ge(f_dev, i * SLOTS + k + 1)
                since(dve, f_out_act, i * SLOTS + k - 1)
                nc.vector.reciprocal(rstd[k % 2][:, :], dev[k % 2][:, :]).then_inc(f_rstd, 1)

            def shift_f(k, i):
                dve.wait_ge(f_rstd, i * SLOTS + k + 1)
                nc.vector.scalar_tensor_tensor(
                    out=shift[k % 2][:, :], in0=mean[k % 2][:, :], scalar=-1.0, in1=rstd[k % 2][:, :], op0=ALU.mult,
                    op1=ALU.mult).then_inc(f_shift, 1)

            def normal_f(js):
                def part(k, i):
                    if js[0] == ACT_LAST:
                        since(dve, f_st[k], i * 16)
                    for j in js:
                        last = nc.vector.tensor_scalar(dout[k][:, j, :], xin[k][:, j, :], mean[k % 2][:, j:j + 1],
                                                       rstd[k % 2][:, j:j + 1], ALU.subtract, ALU.mult)
                    if js[-1] == ROWS - 1:
                        last.then_inc(f_out, 1)
                return part

            over(dve, chunks, SLOTS, (0, rstd_f), (1, stats_f), (0, shift_f), (1, moments_f(0)),
                 (0, normal_f((2, 3))), (1, moments_f(1)), (0, normal_f((4, 5))), (1, moments_f(2)),
                 (0, normal_f((6, 7))))


_INS = ["x", "src", "dst", "edge_attr_128", "L0_gnn_W", "L0_gnn_b", "L1_gnn_W", "L1_gnn_b", "L1_gnn_gamma",
        "L1_gnn_beta"]


def kernel(**inputs):
    import numpy as np
    import concourse.bacc as bacc
    from concourse import mybir as _mybir
    from concourse.bass_utils import run_bass_kernel_spmd

    nc = bacc.Bacc("TRN2", target_bir_lowering=False, num_devices=1)
    arrays, args = {}, []
    for name in _INS:
        a = np.ascontiguousarray(inputs[name])
        arrays[f"in_{name}"] = a
        args.append(nc.dram_tensor(f"in_{name}", a.shape, _mybir.dt.from_np(a.dtype), kind="ExternalInput").ap())
    result = nc.dram_tensor("out_x", inputs["x"].shape, _mybir.dt.float32, kind="ExternalOutput").ap()
    program(nc, *args, result)
    r = run_bass_kernel_spmd(nc, [arrays], core_ids=[0])
    return r.results[0]["out_x"]
```
